# Optimizing a Trainium2 kernel written in Bass

```python
import numpy as np
import jax
import jax.numpy as jnp

def _softmax(x, axis=-1):
    return jax.nn.softmax(x, axis=axis)

def _gelu(x):
    return jax.nn.gelu(x, approximate=True)

def _silu(x):
    return jax.nn.silu(x)

def _sigmoid(x):
    return jax.nn.sigmoid(x)

def _layernorm(x, axis=-1, eps=1e-05):
    m = jnp.mean(x, axis=axis, keepdims=True)
    v = jnp.var(x, axis=axis, keepdims=True)
    return (x - m) / jnp.sqrt(v + eps)

def _scatter_add(tgt, idx, src, axis=0):
    return tgt.at[idx].add(src)

def _segment_sum(src, seg, n):
    return jax.ops.segment_sum(src, seg, n)
kernel_name = 'mk_decoder_preln_d1_seqx_r8_d11416'

def setup_inputs(seed: int=0):
    np.random.seed(seed)
    _w = jnp.asarray

    def _rec_inputs():
        import jax
        import jax.numpy as jnp
        _rk = jax.random.key(seed)
        x = -0.0002928 + 1 * jax.random.normal(jax.random.fold_in(_rk, 1), (32, 64, 128), jnp.float32)
        _lenS = 64 - jax.random.randint(jax.random.fold_in(_rk, 7), (32,), 0, max(1, 64 // 4) + 1, jnp.int32)
        _lenS2 = 64 - jax.random.randint(jax.random.fold_in(_rk, 8), (32,), 0, max(1, 64 // 4) + 1, jnp.int32)
        _ctx_1024P = jax.random.normal(jax.random.fold_in(_rk, 11), (32, 16, 128), jnp.float32)
        _ctx_1024c = jax.random.dirichlet(jax.random.fold_in(_rk, 511), 0.3 * jnp.ones((16,), jnp.float32), (32, 64))
        _ctx_1024t = jnp.einsum('bsk,bkd->bsd', _ctx_1024c, _ctx_1024P)
        _ctx_1024t = _ctx_1024t * jax.lax.rsqrt(jnp.mean(jnp.square(_ctx_1024t)) + 1e-12) * 0.953939
        ctx_1024 = -1.39393e-06 + 0.999914 * (_ctx_1024t + 0.3 * jax.random.normal(jax.random.fold_in(_rk, 611), (32, 64, 128), jnp.float32))
        return (x, ctx_1024)
    x, ctx_1024 = _rec_inputs()

    def _L0_attn_setup():
        import jax, jax.numpy as jnp
        import numpy as np
        B, S, E, H = (4, 256, 128, 16)
        D = E // H

        def _split_heads(x):
            b, s, _ = x.shape
            return x.reshape(b, s, H, D).transpose(0, 2, 1, 3)
        key = jax.random.key(seed)
        ks = jax.random.split(key, 6)
        scale = 1.0 / np.sqrt(E)
        return {'inputs': jax.random.normal(ks[0], (B, S, E), dtype=jnp.float32), 'Wq': jax.random.normal(ks[1], (E, E), dtype=jnp.float32) * scale, 'bq': jnp.zeros((E,), dtype=jnp.float32), 'Wk': jax.random.normal(ks[2], (E, E), dtype=jnp.float32) * scale, 'bk': jnp.zeros((E,), dtype=jnp.float32), 'Wv': jax.random.normal(ks[3], (E, E), dtype=jnp.float32) * scale, 'bv': jnp.zeros((E,), dtype=jnp.float32), 'Wo': jax.random.normal(ks[4], (E, E), dtype=jnp.float32) * scale, 'bo': jnp.zeros((E,), dtype=jnp.float32)}
    _L0_attn_all = _L0_attn_setup()
    _L0_attn_in = {k: v for k, v in _L0_attn_all.items() if k in ('Wq', 'bq', 'Wk', 'bk', 'Wv', 'bv', 'Wo', 'bo')}
    del _L0_attn_all

    def _L0_xattn_setup():
        import jax, jax.numpy as jnp
        import numpy as np
        D_MODEL = 128
        N_HEADS = 16
        HEAD_DIM = D_MODEL // N_HEADS
        key = jax.random.key(seed)
        ks = jax.random.split(key, 12)
        B, S = (2, 256)
        scale = 1.0 / np.sqrt(D_MODEL)
        inp = {'query': jax.random.normal(ks[0], (B, S, D_MODEL), jnp.float32), 'key': jax.random.normal(ks[1], (B, S, D_MODEL), jnp.float32), 'value': jax.random.normal(ks[2], (B, S, D_MODEL), jnp.float32), 'Wq': jax.random.normal(ks[3], (D_MODEL, D_MODEL), jnp.float32) * scale, 'bq': jnp.zeros((D_MODEL,), jnp.float32), 'Wk': jax.random.normal(ks[4], (D_MODEL, D_MODEL), jnp.float32) * scale, 'bk': jnp.zeros((D_MODEL,), jnp.float32), 'Wv': jax.random.normal(ks[5], (D_MODEL, D_MODEL), jnp.float32) * scale, 'bv': jnp.zeros((D_MODEL,), jnp.float32), 'Wo': jax.random.normal(ks[6], (D_MODEL, D_MODEL), jnp.float32) * scale, 'bo': jnp.zeros((D_MODEL,), jnp.float32)}
        return inp
    _L0_xattn_all = _L0_xattn_setup()
    _L0_xattn_in = {k: v for k, v in _L0_xattn_all.items() if k in ('Wq', 'bq', 'Wk', 'bk', 'Wv', 'bv', 'Wo', 'bo')}
    del _L0_xattn_all

    def _L0_ffn_setup():
        import jax, jax.numpy as jnp
        import numpy as np
        E = 8
        TOP_K = 2
        B, S, D = (2, 512, 128)
        H = 512
        CAPACITY = 256

        def _moe(x, Wg, W1, b1, W2, b2):
            b, s, d = x.shape
            xf = x.reshape(b * s, d)
            logits = xf.astype(jnp.float32) @ Wg.astype(jnp.float32)
            probs = jax.nn.softmax(logits, axis=-1)
            vals, idx = jax.lax.top_k(probs, TOP_K)
            w = vals / (jnp.sum(vals, axis=-1, keepdims=True) + 1e-09)
            counts = jnp.zeros((E,), dtype=jnp.int32)
            combine = jnp.zeros((b * s, E), dtype=jnp.float32)
            for k in range(TOP_K):
                oh = jax.nn.one_hot(idx[:, k], E, dtype=jnp.int32)
                pos = jnp.cumsum(oh, axis=0) - 1 + counts[None, :]
                keep = (oh == 1) & (pos < CAPACITY)
                counts = counts + jnp.sum(keep.astype(jnp.int32), axis=0)
                combine = combine + w[:, k][:, None] * keep.astype(jnp.float32)
            out = jnp.zeros_like(xf)
            for e in range(E):
                h = jax.nn.gelu(xf @ W1[e] + b1[e])
                ye = h @ W2[e] + b2[e]
                out = out + combine[:, e][:, None].astype(xf.dtype) * ye
            return out.reshape(b, s, d)
        key = jax.random.key(seed)
        k0, k1, k2, k3 = jax.random.split(key, 4)
        return {'x': jax.random.normal(k0, (B, S, D), dtype=jnp.float32), 'Wg': jax.random.normal(k1, (D, E), dtype=jnp.float32) * 0.02, 'W1': jax.random.normal(k2, (E, D, H), dtype=jnp.float32) * 0.02, 'b1': jnp.zeros((E, H), dtype=jnp.float32), 'W2': jax.random.normal(k3, (E, H, D), dtype=jnp.float32) * 0.02, 'b2': jnp.zeros((E, D), dtype=jnp.float32)}
    _L0_ffn_all = _L0_ffn_setup()
    _L0_ffn_in = {k: v for k, v in _L0_ffn_all.items() if k in ('Wg', 'W1', 'b1', 'W2', 'b2')}
    del _L0_ffn_all
    return {'x': x, 'ctx_1024': ctx_1024, 'L0_attn_Wq': _L0_attn_in['Wq'], 'L0_attn_bq': _L0_attn_in['bq'], 'L0_attn_Wk': _L0_attn_in['Wk'], 'L0_attn_bk': _L0_attn_in['bk'], 'L0_attn_Wv': _L0_attn_in['Wv'], 'L0_attn_bv': _L0_attn_in['bv'], 'L0_attn_Wo': _L0_attn_in['Wo'], 'L0_attn_bo': _L0_attn_in['bo'], 'L0_xattn_Wq': _L0_xattn_in['Wq'], 'L0_xattn_bq': _L0_xattn_in['bq'], 'L0_xattn_Wk': _L0_xattn_in['Wk'], 'L0_xattn_bk': _L0_xattn_in['bk'], 'L0_xattn_Wv': _L0_xattn_in['Wv'], 'L0_xattn_bv': _L0_xattn_in['bv'], 'L0_xattn_Wo': _L0_xattn_in['Wo'], 'L0_xattn_bo': _L0_xattn_in['bo'], 'L0_ffn_Wg': _L0_ffn_in['Wg'], 'L0_ffn_W1': _L0_ffn_in['W1'], 'L0_ffn_b1': _L0_ffn_in['b1'], 'L0_ffn_W2': _L0_ffn_in['W2'], 'L0_ffn_b2': _L0_ffn_in['b2']}

def reference(x, ctx_1024, L0_attn_Wq, L0_attn_bq, L0_attn_Wk, L0_attn_bk, L0_attn_Wv, L0_attn_bv, L0_attn_Wo, L0_attn_bo, L0_xattn_Wq, L0_xattn_bq, L0_xattn_Wk, L0_xattn_bk, L0_xattn_Wv, L0_xattn_bv, L0_xattn_Wo, L0_xattn_bo, L0_ffn_Wg, L0_ffn_W1, L0_ffn_b1, L0_ffn_W2, L0_ffn_b2):
    import jax
    import jax.numpy as jnp

    def _L0_attn_ref(inputs, Wq, bq, Wk, bk, Wv, bv, Wo, bo):
        import jax, jax.numpy as jnp
        import numpy as np
        B, S, E, H = (4, 256, 128, 16)
        D = E // H

        def _split_heads(x):
            b, s, _ = x.shape
            return x.reshape(b, s, H, D).transpose(0, 2, 1, 3)
        q = _split_heads(inputs @ Wq + bq)
        k = _split_heads(inputs @ Wk + bk)
        v = _split_heads(inputs @ Wv + bv)
        inv_sqrt_d = jnp.float32(1.0) / jnp.sqrt(jnp.float32(D))
        scores = jnp.einsum('bhqd,bhkd->bhqk', q, k) * inv_sqrt_d
        weights = jax.nn.softmax(scores, axis=-1)
        attn = jnp.einsum('bhqk,bhkd->bhqd', weights, v)
        attn = attn.transpose(0, 2, 1, 3).reshape(inputs.shape[0], -1, E)
        return attn @ Wo + bo

    def _L0_xattn_ref(query, key, value, Wq, bq, Wk, bk, Wv, bv, Wo, bo):
        import jax, jax.numpy as jnp
        import numpy as np
        D_MODEL = 128
        N_HEADS = 16
        HEAD_DIM = D_MODEL // N_HEADS
        B, S, _ = query.shape
        q = query @ Wq.T + bq
        k = key @ Wk.T + bk
        v = value @ Wv.T + bv
        q = q.reshape(B, S, N_HEADS, HEAD_DIM).transpose(0, 2, 1, 3)
        k = k.reshape(B, S, N_HEADS, HEAD_DIM).transpose(0, 2, 1, 3)
        v = v.reshape(B, S, N_HEADS, HEAD_DIM).transpose(0, 2, 1, 3)
        energy = jnp.einsum('bhqd,bhkd->bhqk', q, k) / jnp.sqrt(jnp.float32(HEAD_DIM))
        attention = jax.nn.softmax(energy, axis=-1)
        x = jnp.einsum('bhqk,bhkd->bhqd', attention, v)
        x = x.transpose(0, 2, 1, 3).reshape(B, S, D_MODEL)
        return x @ Wo.T + bo

    def _L0_ffn_ref(x, Wg, W1, b1, W2, b2):
        import jax, jax.numpy as jnp
        import numpy as np
        E = 8
        TOP_K = 2
        B, S, D = (2, 512, 128)
        H = 512
        CAPACITY = 256

        def _moe(x, Wg, W1, b1, W2, b2):
            b, s, d = x.shape
            xf = x.reshape(b * s, d)
            logits = xf.astype(jnp.float32) @ Wg.astype(jnp.float32)
            probs = jax.nn.softmax(logits, axis=-1)
            vals, idx = jax.lax.top_k(probs, TOP_K)
            w = vals / (jnp.sum(vals, axis=-1, keepdims=True) + 1e-09)
            counts = jnp.zeros((E,), dtype=jnp.int32)
            combine = jnp.zeros((b * s, E), dtype=jnp.float32)
            for k in range(TOP_K):
                oh = jax.nn.one_hot(idx[:, k], E, dtype=jnp.int32)
                pos = jnp.cumsum(oh, axis=0) - 1 + counts[None, :]
                keep = (oh == 1) & (pos < CAPACITY)
                counts = counts + jnp.sum(keep.astype(jnp.int32), axis=0)
                combine = combine + w[:, k][:, None] * keep.astype(jnp.float32)
            out = jnp.zeros_like(xf)
            for e in range(E):
                h = jax.nn.gelu(xf @ W1[e] + b1[e])
                ye = h @ W2[e] + b2[e]
                out = out + combine[:, e][:, None].astype(xf.dtype) * ye
            return out.reshape(b, s, d)
        return _moe(x, Wg, W1, b1, W2, b2)
    x = x + _L0_attn_ref(_layernorm(x, axis=-1), L0_attn_Wq, L0_attn_bq, L0_attn_Wk, L0_attn_bk, L0_attn_Wv, L0_attn_bv, L0_attn_Wo, L0_attn_bo)
    x = x + _L0_xattn_ref(_layernorm(x, axis=-1), ctx_1024, ctx_1024, L0_xattn_Wq, L0_xattn_bq, L0_xattn_Wk, L0_xattn_bk, L0_xattn_Wv, L0_xattn_bv, L0_xattn_Wo, L0_xattn_bo)
    x = x + _L0_ffn_ref(_layernorm(x, axis=-1), L0_ffn_Wg, L0_ffn_W1, L0_ffn_b1, L0_ffn_W2, L0_ffn_b2)
    return x

_drawn_inputs = setup_inputs


def setup_inputs(seed=0):
    import zlib

    import numpy as np

    out = dict(_drawn_inputs(seed))
    spreads = {'L0_attn_bq': (0.0, 0.411),
     'L0_attn_bk': (0.0, 0.8),
     'L0_attn_bv': (0.0, 0.1),
     'L0_attn_bo': (0.0, 0.1),
     'L0_xattn_bq': (0.0, 0.329),
     'L0_xattn_bk': (0.0, 0.8),
     'L0_xattn_bv': (0.0, 0.1),
     'L0_xattn_bo': (0.0, 0.1),
     'L0_ffn_b1': (0.0, 0.754),
     'L0_ffn_b2': (0.0, 0.1)}
    factors = {}
    for name, (base, spread) in spreads.items():
        noise = np.random.default_rng([zlib.crc32(name.encode()), seed]).standard_normal(out[name].shape)
        drawn = base * np.exp(spread * noise) if base else spread * noise
        out[name] = jnp.asarray(drawn.astype(out[name].dtype))
    for name, factor in factors.items():
        out[name] = (out[name] * factor).astype(out[name].dtype)
    return out
```

```python
import concourse.bass as bass
from concourse import mybir
from contextlib import ExitStack

F32 = mybir.dt.float32
BF16 = mybir.dt.bfloat16
I32 = mybir.dt.int32
U32 = mybir.dt.uint32
ALU = mybir.AluOpType
ACT = mybir.ActivationFunctionType
AX = mybir.AxisListType

NSEQ, S, E = 32, 64, 128
H, D = 16, 8
T = NSEQ * S // 128
SPT = 128 // S
UNITS = 2 * T
PAIRS = H // 2
SLOT = 16
SLABS = H * SLOT // 128
GROUPS = 4
EPS = 1e-5
NE, TOP, HID = 8, 2, 512
CAP = 256
HC = HID // 128
BLOCKS = NE * CAP // 128
KT = TOP * T
SCALE = 1.0 / float(D) ** 0.5


def decoder_layer(nc, x_in, ctx_in, wq, wk, wv, wo, bq, bk, bv, bo, ident_in, hmask_in, kone_in, smask_in,
                  consts_in, wg, w1, b1, w2, b2, out):
    ctx = ExitStack()
    with ctx:
        def sb(name, shape, dt=F32):
            return ctx.enter_context(nc.sbuf_tensor(name, shape, dt))

        def bank(name):
            return ctx.enter_context(nc.psum_tensor(name, [128, 512], F32))

        def sem(name):
            return ctx.enter_context(nc.semaphore(name))

        x = sb("x", [128, T // 2, 2, E])
        ctx_ring = sb("ctx_ring", [128, 2, E])
        ident = sb("ident", [128, 128])
        ident_bf = sb("ident_bf", [128, 128], BF16)
        hmask = sb("hmask", [128, 2])
        kone = sb("kone", [128, 1])
        wq_sb = sb("wq_sb", [128, 2, SLABS * 128])
        wk_sb = sb("wk_sb", [128, 2, SLABS * 128])
        wv_sb = sb("wv_sb", [128, 2, E])
        wo_rows = sb("wo_rows", [128, 2, SLABS * 2, E])
        wo_blk = sb("wo_blk", [128, 2, SPT, SLABS * 2, E])
        bq_sb = sb("bq_sb", [128, 2, SLABS])
        bk_sb = sb("bk_sb", [128, 2, SLABS])
        bq_masked = sb("bq_masked", [128, 2, 2, SLABS, SPT])
        smask = sb("smask", [128, SPT])
        key_ones = sb("key_ones", [128, SPT, SLOT])
        bv_col = sb("bv_col", [128, 2, SLABS * 2])
        bv_wide = sb("bv_wide", [128, 2, SLABS * 2, 128])
        bo_rows = sb("bo_rows", [128, 2, E])
        stats = sb("stats", [128, 6])
        meanvar = sb("meanvar", [128, 2, 2])
        logvar = sb("logvar", [128, 2, 1])
        eps_col = sb("eps_col", [128, 1])
        rstd = sb("rstd", [128, 2, 1])
        newton = sb("newton", [128, 2, 5])
        minus_half = sb("minus_half", [128, 1])
        three = sb("three", [128, 1])
        xn = sb("xn", [128, 2, E])
        turned = sb("turned", [128, 2, 2, 128])
        q_bf = sb("q_bf", [128, 2, SLABS, 128], BF16)
        q_blk = sb("q_blk", [128, SLABS, SPT, 2, S])
        k_t = sb("k_t", [128, 2, SLABS, 128])
        k_blk_bf = sb("k_blk_bf", [128, SLABS, SPT, 2, S], BF16)
        v_blk = sb("v_blk", [128, 2, H, SPT, SLOT])
        neg_max = sb("neg_max", [128, H, SLOT], BF16)
        probs = sb("probs", [128, 2, GROUPS, SLABS * 2, S])
        log_den = sb("log_den", [128, SLABS * 2 * S])
        inv_den = sb("inv_den", [128, SLABS * 2 * S])
        den_err = sb("den_err", [128, SLABS * 2 * S])
        neg_inv = sb("neg_inv", [128, SLABS * 2 * S])
        attn_t = sb("attn_t", [128, 2, SLABS * 2, S])

        tri = sb("tri", [128, 128])
        tri_bf = sb("tri_bf", [128, 128], BF16)
        count_row = sb("count_row", [128, 128])
        count_bf = sb("count_bf", [128, 128], BF16)
        small = sb("small", [128, 2 * NE + BLOCKS + 2 * KT + 1])
        rank = small[:, 0:NE]
        expert_no = small[:, NE:2 * NE]
        block_no = small[:, 2 * NE:2 * NE + BLOCKS]
        tile_no = small[:, 2 * NE + BLOCKS:2 * NE + BLOCKS + KT]
        choice_no = small[:, 2 * NE + BLOCKS + KT:2 * NE + BLOCKS + 2 * KT]
        part_no = small[:, 2 * NE + BLOCKS + 2 * KT:]
        ones_bf = sb("ones_bf", [128, 128], BF16)
        wg_sb = sb("wg_sb", [128, NE])
        w1_sb = sb("w1_sb", [128, NE, HID])
        b1_sb = sb("b1_sb", [128, NE, HC])
        w2_sb = sb("w2_sb", [128, NE, HC, E])
        b2_rows = sb("b2_rows", [128, NE, E])
        zeros = sb("zeros", [128, 1024])
        stats3 = sb("stats3", [128, T, 6])
        meanvar3 = sb("meanvar3", [128, T, 2])
        rstd3 = sb("rstd3", [128, 5, T])
        xn3 = sb("xn3", [128, T, E])
        xt3 = sb("xt3", [128, T, 128])
        gate = sb("gate", [128, T, NE])
        gate_tmp = sb("gate_tmp", [128, T, NE])
        gate_col = sb("gate_col", [128, 4, T])
        best = sb("best", [128, TOP, T])
        chosen = sb("chosen", [128, TOP, T, NE], BF16)
        first_count = sb("first_count", [128, NE])
        first_count_bf = sb("first_count_bf", [128, NE], BF16)
        base = sb("base", [128, TOP, NE])
        order = sb("order", [128, TOP, T, NE])
        order_tmp = sb("order_tmp", [128, TOP, T, NE])
        place = sb("place", [128, KT])
        expert = sb("expert", [128, KT])
        upper = sb("upper", [128, KT])
        row_in = sb("row_in", [128, KT])
        blk = sb("blk", [128, KT])
        dropped = sb("dropped", [128, KT])
        kept = sb("kept", [128, KT])
        in_block = sb("in_block", [128, KT, BLOCKS])
        at_row = sb("at_row", [128, KT, 128], BF16)
        facts = sb("facts", [128, KT, 4, BLOCKS], BF16)
        table = sb("table", [128, 4, BLOCKS])
        src_f = sb("src_f", [128, BLOCKS])
        dst_f = sb("dst_f", [128, BLOCKS])
        src_row = sb("src_row", [128, BLOCKS], U32)
        dst_row = sb("dst_row", [128, BLOCKS], U32)
        xe = sb("xe", [128, BLOCKS, E])
        xe_t = sb("xe_t", [128, NE, CAP])
        hid = sb("hid", [128, 2, HC, CAP])
        ye = sb("ye", [128, BLOCKS, E])
        z = sb("z", [128, TOP, T, E])
        xn_rows = nc.dram_tensor("xn_rows", (NSEQ * S, E), F32).ap()
        z_rows = nc.dram_tensor("z_rows", (TOP * NSEQ * S, E), F32).ap()

        ps_q = [bank("ps_q0"), bank("ps_q1")]
        ps_kv = bank("ps_kv")
        ps_s = [bank("ps_s%d" % g) for g in range(GROUPS)]
        ps_m = bank("ps_m")

        ld_const = sem("ld_const")
        ld_w = sem("ld_w")
        ld_x = [sem("ld_x%d" % i) for i in range(4)]
        ld_ctx = [sem("ld_ctx0"), sem("ld_ctx1")]
        st_out = sem("st_out")
        prep_pool = sem("prep_pool")
        prep_dve = sem("prep_dve")
        prep_pe = sem("prep_pe")
        prep_act = sem("prep_act")
        bias_added = sem("bias_added")
        stats_done = sem("stats_done")
        aggr_done = sem("aggr_done")
        logvar_done = sem("logvar_done")
        rstd0_done = sem("rstd0_done")
        newton_done = sem("newton_done")
        xn_done = sem("xn_done")
        turns_done = sem("turns_done")
        turned_copied = sem("turned_copied")
        proj_done = sem("proj_done")
        kt_done = sem("kt_done")
        qbf_done = sem("qbf_done")
        kbf_done = sem("kbf_done")
        v_done = sem("v_done")
        s_done = sem("s_done")
        max_done = sem("max_done")
        inject_done = sem("inject_done")
        qblk_done = sem("qblk_done")
        st_done = sem("st_done")
        exp_done = sem("exp_done")
        av_done = sem("av_done")
        logden_done = sem("logden_done")
        inv0_done = sem("inv0_done")
        refine_done = sem("refine_done")
        attn_done = sem("attn_done")
        y_done = sem("y_done")
        resid_done = sem("resid_done")

        ld_gate = sem("ld_gate")
        gate_prep = sem("gate_prep")
        ld_expert = sem("ld_expert")
        z_zero = sem("z_zero")
        z_cleared = sem("z_cleared")
        st_xn = sem("st_xn")
        gathered = [sem("gathered%d" % i) for i in range(BLOCKS)]
        st_z = sem("st_z")
        ld_z = [sem("ld_z%d" % i) for i in range(4)]
        stats3_done = sem("stats3_done")
        rstd3_done = sem("rstd3_done")
        newton3_done = sem("newton3_done")
        xn3_done = sem("xn3_done")
        turns3_done = sem("turns3_done")
        xt3_done = sem("xt3_done")
        logits_done = sem("logits_done")
        shifted_done = sem("shifted_done")
        gate_exp_done = sem("gate_exp_done")
        route = sem("route")
        total_done = sem("total_done")
        queue_done = sem("queue_done")
        facts_done = sem("facts_done")
        table_done = sem("table_done")
        rows_done = sem("rows_done")
        xe_turned = sem("xe_turned")
        xet_done = sem("xet_done")
        up_done = sem("up_done")
        gelu_done = sem("gelu_done")
        down_done = sem("down_done")
        ye_done = sem("ye_done")
        out_done = sem("out_done")

        block = ctx.enter_context(nc.Block())
        ps_x = [ps_kv, ps_m]
        ps_y = ps_q

        class Unit:

            def __init__(self, number, pair=None):
                self.number, self.pair = number, pair
                self.par = number % 2
                self.layer = number // T

            def at(self, k):
                return Unit(self.number + k, self.pair)

            @property
            def exists(self):
                return 0 <= self.number < UNITS

            def tile_pair(self):
                p = (self.number % T) // 2
                return p if self.pair is None else self.pair + p

            def x(self):
                return x[:, self.tile_pair(), self.par, :]

            def count(self, per, extra=0):
                n = per * self.number + extra
                return n if self.pair is None else self.pair * (2 * per) + n

        def wait(eng, semaphore, unit, per, extra=0):
            if unit.pair is None:
                if unit.count(per, extra) > 0:
                    eng.wait_ge(semaphore, unit.count(per, extra))
            else:
                eng.wait_ge(semaphore, unit.count(per, extra))

        FIRST, LAST = -3, UNITS + 1
        LOOP_FROM, LOOP_STEPS = 2, 10

        def run_steps(eng, step):
            n = FIRST
            while n <= LAST:
                if n % T == LOOP_FROM and 0 <= n < UNITS:
                    with eng.Fori(0, LOOP_STEPS // 2) as pair:
                        for k in range(2):
                            step(Unit(n + k, pair))
                    n += LOOP_STEPS
                else:
                    step(Unit(n))
                    n += 1

        @block.sync
        def _(sp):
            x_tiles = x_in.rearrange("(i k p) e -> p i k e", k=2, p=128)
            ctx_tiles = ctx_in.rearrange("(i k p) e -> p i k e", k=2, p=128)
            for q in range(4):
                sp.dma_start(x[:, 2 * q:2 * q + 2], x_tiles[:, 2 * q:2 * q + 2]).then_inc(ld_x[q], 16)

            sp.dma_start(wg_sb[:], wg).then_inc(ld_gate, 16)
            sp.dma_start(tri[:], consts_in[:, 0:128]).then_inc(ld_gate, 16)
            sp.dma_start(count_row[:], consts_in[:, 128:256]).then_inc(ld_gate, 16)
            sp.dma_start(small[:], consts_in[:, 256:]).then_inc(ld_gate, 16)

            def load_ctx(u):
                wait(sp, turns_done, u, 1, -1)
                sp.dma_start(ctx_ring[:, u.par, :], ctx_tiles[:, u.tile_pair(), u.par, :])\
                  .then_inc(ld_ctx[u.par], 16)

            for t in range(2):
                load_ctx(Unit(T + t))
            with sp.Fori(0, T // 2 - 1) as pair:
                for k in range(2):
                    load_ctx(Unit(T + 2 + k, pair))
            xn_tiles = xn_rows.rearrange("(t p) e -> p t e", p=128)
            for q in range(4):
                sp.wait_ge(xn3_done, 4 * q + 4)
                sp.dma_start(xn_tiles[:, 4 * q:4 * q + 4], xn3[:, 4 * q:4 * q + 4]).then_inc(st_xn, 16)
            z_tiles = z_rows.rearrange("(k t p) e -> p k t e", k=TOP, p=128)
            sp.wait_ge(st_z, 16 * BLOCKS)
            for q in range(4):
                tiles = slice(4 * q, 4 * q + 4)
                for k in range(TOP):
                    sp.dma_start(z[:, k, tiles], z_tiles[:, k, tiles]).then_inc(ld_z[q], 16)
            out_tiles = out.rearrange("(i k p) e -> p i k e", k=2, p=128)
            for q in range(4):
                sp.wait_ge(out_done, 8 * q + 8)
                sp.dma_start(out_tiles[:, 2 * q:2 * q + 2], x[:, 2 * q:2 * q + 2]).then_inc(st_out, 16)
            sp.wait_ge(st_out, 64)

        @block.gpsimd
        def _(pool):
            nc.gpsimd.memset(zeros[:], 0.0).then_inc(z_zero, 1)
            nc.gpsimd.memset(ones_bf[:], 1.0).then_inc(z_zero, 1)
            nc.gpsimd.memset(v_blk[:], 0.0).then_inc(prep_pool, 1)
            nc.gpsimd.memset(neg_max[:], 0.0).then_inc(prep_pool, 1)
            nc.gpsimd.memset(key_ones[:], 0.0).then_inc(prep_pool, 1)
            nc.gpsimd.memset(eps_col[:], EPS).then_inc(prep_pool, 1)
            nc.gpsimd.memset(minus_half[:], -0.5).then_inc(prep_pool, 1)
            nc.gpsimd.memset(three[:], 3.0).then_inc(prep_pool, 1)
            for b in range(SPT):
                pool.wait_ge(prep_pool, 6 + b)
                nc.gpsimd.memset(key_ones[S * b:S * b + S, b, :], 1.0).then_inc(prep_pool, 1)
            pool.wait_ge(prep_pool, 8)

            def step(n):
                u, old = n.at(3), n.at(2)
                if u.exists:
                    v, yy, vyy, less3, half = (newton[:, u.par, i:i + 1] for i in range(5))
                    y = rstd[:, u.par, :]
                    wait(pool, rstd0_done, u, 1, 1)
                    nc.gpsimd.tensor_tensor(v, meanvar[:, u.par, 1:2], eps_col[:], ALU.add)\
                      .then_inc(newton_done, 1)
                    nc.gpsimd.tensor_tensor(yy, y, y, ALU.mult).then_inc(newton_done, 1)
                    nc.gpsimd.tensor_tensor(half, y, minus_half[:], ALU.mult).then_inc(newton_done, 1)
                    wait(pool, newton_done, u, 6, 3)
                    nc.gpsimd.tensor_tensor(vyy, yy, v, ALU.mult).then_inc(newton_done, 1)
                    wait(pool, newton_done, u, 6, 4)
                    nc.gpsimd.tensor_tensor(less3, vyy, three[:], ALU.subtract).then_inc(newton_done, 1)
                    wait(pool, newton_done, u, 6, 5)
                    nc.gpsimd.tensor_tensor(y, less3, half, ALU.mult).then_inc(newton_done, 1)
                if old.exists:
                    wait(pool, xn_done, old, 1, 1)
                    nc.gpsimd.tensor_tensor(old.x(), old.x(), bo_rows[:, old.layer, :], ALU.add)\
                      .then_inc(bias_added, 1)

            pool.wait_ge(z_zero, 2)
            z_flat = z_rows.rearrange("(c p r) e -> c p (r e)", p=128, r=8)
            for c in range(TOP * NSEQ * S // 1024):
                pool.dma_start(z_flat[c], zeros[:]).then_inc(z_cleared, 16)
            pool.dma_start(w1_sb[:], w1.rearrange("x d h -> d x h")).then_inc(ld_expert, 16)
            pool.dma_start(w2_sb[:], w2.rearrange("x (c p) e -> p x c e", p=128)).then_inc(ld_expert, 16)
            pool.dma_start(b1_sb[:], b1).then_inc(ld_expert, 16)
            pool.dma_start(b2_rows[:], b2.rearrange("(q x) e -> q x e", q=1).to_broadcast([128, NE, E]))\
                .then_inc(ld_expert, 16)

            run_steps(pool, step)

            v, t0, t1, y, y1 = (rstd3[:, i, :] for i in range(5))
            pool.wait_ge(rstd3_done, 2)
            nc.gpsimd.tensor_scalar(v, meanvar3[:, :, 1], EPS, None, ALU.add).then_inc(newton3_done, 1)
            nc.gpsimd.tensor_tensor(t0, y, y, ALU.mult).then_inc(newton3_done, 1)
            pool.wait_ge(newton3_done, 2)
            nc.gpsimd.tensor_tensor(t0, t0, v, ALU.mult).then_inc(newton3_done, 1)
            pool.wait_ge(newton3_done, 3)
            nc.gpsimd.tensor_scalar(t1, t0, -0.5, 1.5, ALU.mult, ALU.add).then_inc(newton3_done, 1)
            pool.wait_ge(newton3_done, 4)
            nc.gpsimd.tensor_tensor(y1, y, t1, ALU.mult).then_inc(newton3_done, 1)
            pool.wait_ge(rows_done, 2)
            pool.wait_ge(st_xn, 64)
            for i in range(BLOCKS):
                pool.indirect_dma_start(out=xe[:, i, :], out_offset=None, in_=xn_rows,
                                        in_offset=bass.IndirectOffsetOnAxis(ap=src_row[:, i:i + 1], axis=0))\
                    .then_inc(gathered[i], 16)
            pool.wait_ge(z_cleared, 16 * (TOP * NSEQ * S // 1024))
            for i in range(BLOCKS):
                pool.wait_ge(ye_done, i // 2 + 1)
                pool.indirect_dma_start(out=z_rows,
                                        out_offset=bass.IndirectOffsetOnAxis(ap=dst_row[:, i:i + 1], axis=0),
                                        in_=ye[:, i, :], in_offset=None,
                                        bounds_check=TOP * NSEQ * S - 1, oob_is_err=False)\
                    .then_inc(st_z, 16)

        @block.vector
        def _(dve):
            dve.wait_ge(ld_const, 64)
            nc.vector.tensor_copy(ident_bf[:], ident[:]).then_inc(prep_dve, 1)
            dve.wait_ge(ld_w, 128)
            for a in range(2):
                nc.vector.tensor_scalar(bk_sb[:, a, :], bk_sb[:, a, :], kone[:, 0:1], None, ALU.add)\
                  .then_inc(prep_dve, 1)
                for j in range(SLABS * 2):
                    nc.vector.tensor_copy(bv_wide[:, a, j, :],
                                          bv_col[:, a, j:j + 1].to_broadcast([128, 128])).then_inc(prep_dve, 1)
                for hh in range(2):
                    nc.vector.tensor_scalar(bq_masked[:, a, hh],
                                            bq_sb[:, a, :].unsqueeze(2).to_broadcast([128, SLABS, SPT]),
                                            hmask[:, hh:hh + 1], None, ALU.mult).then_inc(prep_dve, 1)
            dve.wait_ge(prep_pe, 1)
            for a in range(2):
                nc.vector.tensor_tensor(bo_rows[:, a, :], bo_rows[:, a, :],
                                        ps_kv[:, a * E:a * E + E], ALU.add).then_inc(prep_dve, 1)
            dve.wait_ge(prep_dve, 17)
            dve.wait_ge(ld_gate, 64)
            nc.vector.tensor_copy(tri_bf[:], tri[:]).then_inc(gate_prep, 1)
            nc.vector.tensor_copy(count_bf[:], count_row[:]).then_inc(gate_prep, 1)

            def step(n):
                ln, nxt, prev, old = n.at(3), n.at(1), n.at(-1), n.at(-2)
                if ln.exists:
                    if ln.layer == 0:
                        if ln.pair is None:
                            dve.wait_ge(ld_x[ln.number // 4], 16)
                        else:
                            for q in ld_x:
                                dve.wait_ge(q, 16)
                    else:
                        wait(dve, resid_done, ln, 1, -T + 1)
                    wait(dve, aggr_done, ln, 1, 0)
                    nc.vector.bn_stats(stats[:], ln.x()).then_inc(stats_done, 1)
                def group_max(g):
                    wait(dve, s_done, n, GROUPS, g + 1)
                    nc.vector.tensor_reduce(
                        neg_max[:].rearrange("p (s g j) c -> p s g j c", s=SLABS, g=GROUPS)[:, :, g, :, D],
                        ps_s[g][:, 0:SLABS * 2 * S].rearrange("p (s j k) -> p s j k", s=SLABS, k=S),
                        AX.X, ALU.max, negate=True).then_inc(max_done, 1)

                if n.exists:
                    if n.number == 0:
                        dve.wait_ge(prep_pool, 8)
                    wait(dve, inject_done, n, 1, 0)
                    group_max(0)
                if ln.exists:
                    wait(dve, stats_done, ln, 1, 1)
                    wait(dve, xn_done, ln, 1, -1)
                if n.exists:
                    group_max(1)
                if ln.exists:
                    nc.vector.bn_aggr(meanvar[:, ln.par, :], stats[:]).then_inc(aggr_done, 1)
                if n.exists:
                    group_max(2)
                    group_max(3)
                if old.exists:
                    wait(dve, y_done, old, 1, 1)
                    wait(dve, bias_added, old, 1, 1)
                    nc.vector.tensor_tensor(old.x(), old.x(), ps_m[:, 0:E], ALU.add)\
                      .then_inc(resid_done, 1)
                if n.exists:
                    wait(dve, inject_done, n, 1, 1)
                    for hh in range(2):
                        nc.vector.scalar_tensor_tensor(
                            out=q_blk[:, :, :, hh, :],
                            in0=ps_q[n.par][:, 0:SLABS * 128].rearrange("p (s b t) -> p s b t", s=SLABS, b=SPT),
                            scalar=hmask[:, hh:hh + 1],
                            in1=bq_masked[:, n.layer, hh].unsqueeze(3).to_broadcast([128, SLABS, SPT, S]),
                            op0=ALU.mult, op1=ALU.add).then_inc(qblk_done, 1)
                if nxt.exists:
                    wait(dve, proj_done, nxt, 1, 1)
                    nc.vector.tensor_tensor(
                        q_bf[:, nxt.par], ps_q[nxt.par][:, 0:SLABS * 128].rearrange("p (s t) -> p s t", s=SLABS),
                        bq_sb[:, nxt.layer, :].unsqueeze(2).to_broadcast([128, SLABS, 128]),
                        ALU.add).then_inc(qbf_done, 1)
                    wait(dve, kt_done, nxt, SLABS, SLABS)
                    wait(dve, s_done, n, GROUPS, GROUPS)
                    for hh in range(2):
                        nc.vector.tensor_scalar(
                            k_blk_bf[:, :, :, hh, :],
                            k_t[:, nxt.par].rearrange("p s (b t) -> p s b t", b=SPT),
                            hmask[:, hh:hh + 1], None, ALU.mult).then_inc(kbf_done, 1)
                if prev.exists:
                    wait(dve, av_done, prev, 1, 1)
                    wait(dve, inv0_done, prev, 1, 1)
                    nc.vector.tensor_tensor(den_err[:], ps_m[:, 256:512], inv_den[:], ALU.mult)\
                      .then_inc(refine_done, 1)
                    wait(dve, refine_done, prev, 2, 1)
                    nc.vector.scalar_tensor_tensor(out=neg_inv[:], in0=den_err[:], scalar=2.0, in1=inv_den[:],
                                                   op0=ALU.subtract, op1=ALU.mult).then_inc(refine_done, 1)
                    wait(dve, refine_done, prev, 2, 2)
                    nc.vector.scalar_tensor_tensor(
                        out=attn_t[:, prev.par].rearrange("p j q -> p (j q)"), in0=ps_m[:, 0:256],
                        scalar=-1.0, in1=neg_inv[:], op0=ALU.mult, op1=ALU.mult).then_inc(attn_done, 1)
                if ln.exists:
                    wait(dve, newton_done, ln, 6, 6)
                    wait(dve, turns_done, ln, 1, -1)
                    nc.vector.tensor_scalar(xn[:, ln.par, :], ln.x(), meanvar[:, ln.par, 0:1],
                                            rstd[:, ln.par, :], ALU.subtract, ALU.mult).then_inc(xn_done, 1)

            run_steps(dve, step)

            for t in range(T):
                dve.wait_ge(resid_done, T + t + 1)
                nc.vector.bn_stats(stats3[:, t, :], x[:, t // 2, t % 2, :]).then_inc(stats3_done, 1)
            for t in range(T):
                dve.wait_ge(stats3_done, t + 1)
                nc.vector.bn_aggr(meanvar3[:, t, :], stats3[:, t, :]).then_inc(stats3_done, 1)
            dve.wait_ge(newton3_done, 5)
            for t in range(T):
                nc.vector.tensor_scalar(xn3[:, t, :], x[:, t // 2, t % 2, :], meanvar3[:, t, 0:1],
                                        rstd3[:, 4, t:t + 1], ALU.subtract, ALU.mult).then_inc(xn3_done, 1)
            for q in range(2):
                dve.wait_ge(turns3_done, 2 * q + 2)
                nc.vector.tensor_copy(xt3[:, 8 * q + 4:8 * q + 8, :],
                                      ps_s[2 * q + 1][:].rearrange("p (t n) -> p t n", n=128))\
                    .then_inc(xt3_done, 1)

            steps = [0]

            def then(ins):
                steps[0] += 1
                ins.then_inc(route, 1)
                dve.wait_ge(route, steps[0])

            def wide(col):
                return col.unsqueeze(2).to_broadcast([128, T, NE])

            dve.wait_ge(logits_done, 1)
            logits = ps_q[0][:, 0:T * NE].rearrange("p (t e) -> p t e", e=NE)
            then(nc.vector.tensor_reduce(gate_col[:, 0], logits, AX.X, ALU.max))
            nc.vector.tensor_tensor(gate[:], logits, wide(gate_col[:, 0]), ALU.subtract)\
                .then_inc(shifted_done, 1)
            dve.wait_ge(gate_exp_done, 1)
            then(nc.vector.tensor_reduce(gate_col[:, 1], gate[:], AX.X, ALU.add))
            then(nc.vector.reciprocal(gate_col[:, 2], gate_col[:, 1]))
            then(nc.vector.tensor_tensor(gate[:], gate[:], wide(gate_col[:, 2]), ALU.mult))
            for k in range(TOP):
                then(nc.vector.tensor_reduce(best[:, k, :], gate[:], AX.X, ALU.max))
                then(nc.vector.tensor_tensor(gate_tmp[:], gate[:], wide(best[:, k, :]), ALU.is_equal))
                then(nc.vector.tensor_tensor(gate_tmp[:], gate_tmp[:],
                                             rank.unsqueeze(1).to_broadcast([128, T, NE]), ALU.mult))
                then(nc.vector.tensor_reduce(gate_col[:, 3], gate_tmp[:], AX.X, ALU.max))
                then(nc.vector.tensor_tensor(chosen[:, k], gate_tmp[:], wide(gate_col[:, 3]), ALU.is_equal))
                if k == 0:
                    then(nc.vector.scalar_tensor_tensor(out=gate[:], in0=chosen[:, 0], scalar=-2.0, in1=gate[:],
                                                        op0=ALU.mult, op1=ALU.add))
                    then(nc.vector.tensor_reduce(first_count[:], chosen[:, 0].rearrange("p t e -> p e t"),
                                                 AX.X, ALU.add))
                    nc.vector.tensor_copy(first_count_bf[:], first_count[:]).then_inc(total_done, 1)
                else:
                    nc.vector.tensor_copy(base[:, 0, :], zeros[:, 0:NE]).then_inc(total_done, 1)
            then(nc.vector.tensor_tensor(gate_col[:, 0], best[:, 0, :], best[:, 1, :], ALU.add))
            then(nc.vector.tensor_scalar(gate_col[:, 1], gate_col[:, 0], 1e-9, None, ALU.add))
            then(nc.vector.reciprocal(gate_col[:, 2], gate_col[:, 1]))
            then(nc.vector.tensor_tensor(best[:], best[:],
                                         gate_col[:, 2].unsqueeze(1).to_broadcast([128, TOP, T]), ALU.mult))
            then(nc.vector.tensor_tensor(order_tmp[:].rearrange("p k t e -> p (k t) e"),
                                         chosen[:].rearrange("p k t e -> p (k t) e"),
                                         expert_no.unsqueeze(1).to_broadcast([128, KT, NE]), ALU.mult))
            then(nc.vector.tensor_reduce(expert[:], order_tmp[:].rearrange("p k t e -> p (k t) e"), AX.X, ALU.add))
            dve.wait_ge(queue_done, 1)
            then(nc.vector.tensor_scalar(base[:, 1, :], ps_kv[:, 0:NE], float(CAP), None, ALU.min))
            then(nc.vector.tensor_tensor(order[:], ps_q[1][:, 0:KT * NE].rearrange("p (k t e) -> p k t e", t=T, e=NE),
                                         base[:].unsqueeze(2).to_broadcast([128, TOP, T, NE]), ALU.add))
            then(nc.vector.tensor_tensor(order[:], order[:], chosen[:], ALU.mult))
            then(nc.vector.tensor_reduce(place[:], order[:].rearrange("p k t e -> p (k t) e"), AX.X, ALU.add))
            then(nc.vector.tensor_scalar(upper[:], place[:], 128.5, None, ALU.is_gt))
            then(nc.vector.scalar_tensor_tensor(out=row_in[:], in0=upper[:], scalar=-128.0, in1=place[:],
                                                op0=ALU.mult, op1=ALU.add))
            then(nc.vector.tensor_scalar(dropped[:], place[:], CAP + 0.5, None, ALU.is_gt))
            then(nc.vector.scalar_tensor_tensor(out=blk[:], in0=expert[:], scalar=float(CAP // 128), in1=upper[:],
                                                op0=ALU.mult, op1=ALU.add))
            then(nc.vector.scalar_tensor_tensor(out=blk[:], in0=dropped[:], scalar=float(4 * BLOCKS), in1=blk[:],
                                                op0=ALU.mult, op1=ALU.add))
            then(nc.vector.tensor_scalar(kept[:], dropped[:], -1.0, 1.0, ALU.mult, ALU.add))
            then(nc.vector.tensor_tensor(best[:], best[:], kept[:].rearrange("p (k t) -> p k t", k=TOP), ALU.mult))
            then(nc.vector.tensor_tensor(in_block[:], block_no.unsqueeze(1).to_broadcast([128, KT, BLOCKS]),
                                         blk[:].unsqueeze(2).to_broadcast([128, KT, BLOCKS]), ALU.is_equal))
            nc.vector.tensor_scalar(facts[:, :, 0, :], in_block[:], part_no, None, ALU.mult)\
                .then_inc(facts_done, 1)
            nc.vector.tensor_tensor(facts[:, :, 1, :], in_block[:],
                                    tile_no.unsqueeze(2).to_broadcast([128, KT, BLOCKS]), ALU.mult)\
                .then_inc(facts_done, 1)
            nc.vector.tensor_tensor(facts[:, :, 2, :], in_block[:],
                                    choice_no.unsqueeze(2).to_broadcast([128, KT, BLOCKS]), ALU.mult)\
                .then_inc(facts_done, 1)
            nc.vector.tensor_copy(facts[:, :, 3, :], in_block[:]).then_inc(facts_done, 1)
            for i in range(KT):
                nc.vector.tensor_scalar(at_row[:, i, :], count_bf[:], row_in[:, i:i + 1], None, ALU.is_equal)\
                    .then_inc(facts_done, 1)
            dve.wait_ge(table_done, 1)
            then(nc.vector.tensor_copy(table[:], ps_m[:, 0:4 * BLOCKS].rearrange("p (v i) -> p v i", v=4)))
            then(nc.vector.scalar_tensor_tensor(out=src_f[:], in0=table[:, 1], scalar=128.0, in1=table[:, 0],
                                                op0=ALU.mult, op1=ALU.add))
            nc.vector.tensor_copy(src_row[:], src_f[:]).then_inc(rows_done, 1)
            then(nc.vector.tensor_scalar(dst_f[:], table[:, 3], -8192.0, 8192.0, ALU.mult, ALU.add))
            then(nc.vector.tensor_tensor(dst_f[:], dst_f[:], src_f[:], ALU.add))
            then(nc.vector.scalar_tensor_tensor(out=dst_f[:], in0=table[:, 2], scalar=float(NSEQ * S), in1=dst_f[:],
                                                op0=ALU.mult, op1=ALU.add))
            nc.vector.tensor_copy(dst_row[:], dst_f[:]).then_inc(rows_done, 1)

            def expert_tokens(e):
                dve.wait_ge(xe_turned, e + 1)
                nc.vector.tensor_copy(xe_t[:, e, :], ps_x[e % 2][:, 0:CAP]).then_inc(xet_done, 1)

            def expert_answer(e):
                dve.wait_ge(down_done, e + 1)
                nc.vector.tensor_tensor(ye[:, 2 * e:2 * e + 2, :],
                                        ps_y[e % 2][:, 0:2 * E].rearrange("p (i n) -> p i n", i=2),
                                        b2_rows[:, e:e + 1, :].to_broadcast([128, 2, E]), ALU.add)\
                    .then_inc(ye_done, 1)

            dve.wait_ge(ld_expert, 64)
            for e in range(NE + 2):
                if e < NE:
                    expert_tokens(e)
                if e >= 2:
                    expert_answer(e - 2)
            for q in range(4):
                dve.wait_ge(ld_z[q], 32)
                for k in range(TOP):
                    for t in range(4 * q, 4 * q + 4):
                        if k:
                            dve.wait_ge(out_done, 8 * q + t % 4 + 1)
                        row = x[:, t // 2, t % 2, :]
                        nc.vector.scalar_tensor_tensor(out=row, in0=z[:, k, t, :], scalar=best[:, k, t:t + 1],
                                                       in1=row, op0=ALU.mult, op1=ALU.add).then_inc(out_done, 1)

        @block.scalar
        def _(act):
            act.dma_start(ident[:], ident_in).then_inc(ld_const, 16)
            act.dma_start(hmask[:], hmask_in).then_inc(ld_const, 16)
            act.dma_start(kone[:], kone_in).then_inc(ld_const, 16)
            act.dma_start(smask[:], smask_in).then_inc(ld_const, 16)
            act.dma_start(wo_rows[:], wo).then_inc(ld_w, 16)
            for dst, src in ((wq_sb, wq), (wk_sb, wk), (wv_sb, wv)):
                act.dma_start(dst[:], src.rearrange("a e n -> e a n")).then_inc(ld_w, 16)
            act.dma_start(bq_sb[:], bq).then_inc(ld_w, 16)
            act.dma_start(bk_sb[:], bk).then_inc(ld_w, 16)
            act.dma_start(bv_col[:], bv).then_inc(ld_w, 16)
            act.dma_start(bo_rows[:], bo.rearrange("(q a) n -> q a n", q=1).to_broadcast([128, 2, E]))\
               .then_inc(ld_w, 16)

            act.preload_act_table_set("natural_log_exp_and_others")
            act.wait_ge(ld_const, 64)
            act.wait_ge(ld_w, 128)
            for a in range(2):
                for b in range(SPT):
                    act.activation(wo_blk[:, a, b], wo_rows[:, a], ACT.Copy, scale=smask[:, b:b + 1])\
                       .then_inc(prep_act, 1)

            act.wait_ge(prep_pool, 8)

            def step(n):
                nxt, prev, ln = n.at(1), n.at(-1), n.at(3)
                if nxt.exists:
                    wait(act, turns_done, nxt, 1, 1)
                    wait(act, proj_done, nxt, 1, -1)
                    act.activation(turned[:, nxt.par, 0:1 + nxt.layer, :],
                                   ps_q[nxt.par][:, 256:256 + 128 * (1 + nxt.layer)].rearrange(
                                       "p (j t) -> p j t", t=128), ACT.Copy).then_inc(turned_copied, 1)
                    wait(act, proj_done, nxt, 1, 1)
                    wait(act, st_done, nxt, GROUPS, -GROUPS)
                    if n.number <= 1:
                        act.wait_ge(prep_dve, 17)
                    for s in range(SLABS):
                        act.activation(k_t[:, nxt.par, s, :], ps_kv[:, 128 * s:128 * s + 128],
                                       ACT.Identity, bias=bk_sb[:, nxt.layer, s:s + 1]).then_inc(kt_done, 1)
                    wait(act, av_done, n, 1, 0)
                    for b in range(SPT):
                        rows = slice(S * b, S * b + S)
                        act.activation(v_blk[rows, nxt.par, :, b, 0:D],
                                       ps_kv[rows, SLABS * 128:SLABS * 128 + 128].rearrange(
                                           "p (h d) -> p h d", d=D), ACT.Copy).then_inc(v_done, 1)
                if ln.exists:
                    wait(act, aggr_done, ln, 1, 1)
                    act.activation(logvar[:, ln.par, :], meanvar[:, ln.par, 1:2], ACT.Ln,
                                   bias=eps_col[:, 0:1]).then_inc(logvar_done, 1)
                if prev.exists:
                    wait(act, av_done, prev, 1, 1)
                    act.activation(log_den[:], ps_m[:, 256:512], ACT.Ln).then_inc(logden_done, 1)
                if ln.exists:
                    wait(act, logvar_done, ln, 1, 1)
                    act.activation(rstd[:, ln.par, :], logvar[:, ln.par, :], ACT.Exp, scale=-0.5)\
                       .then_inc(rstd0_done, 1)
                if prev.exists:
                    wait(act, logden_done, prev, 1, 1)
                    act.activation(inv_den[:], log_den[:], ACT.Exp, scale=-1.0).then_inc(inv0_done, 1)
                if n.exists:
                    for g in range(GROUPS):
                        wait(act, st_done, n, GROUPS, g + 1)
                        act.activation(probs[:, n.par, g], ps_s[g][:, 0:SLABS * 2 * S].rearrange(
                            "p (j q) -> p j q", q=S), ACT.Exp, scale=SCALE)\
                           .then_inc(exp_done, 1)

            run_steps(act, step)

            act.wait_ge(stats3_done, 2 * T)
            act.activation(rstd3[:, 0, :], meanvar3[:, :, 1], ACT.Ln, bias=eps_col[:, 0:1]).then_inc(rstd3_done, 1)
            act.wait_ge(rstd3_done, 1)
            act.activation(rstd3[:, 3, :], rstd3[:, 0, :], ACT.Exp, scale=-0.5).then_inc(rstd3_done, 1)
            for q in range(2):
                act.wait_ge(turns3_done, 2 * q + 1)
                act.activation(xt3[:, 8 * q:8 * q + 4, :], ps_s[2 * q][:].rearrange("p (t n) -> p t n", n=128),
                               ACT.Copy).then_inc(xt3_done, 1)
            act.wait_ge(shifted_done, 1)
            act.activation(gate[:], gate[:], ACT.Exp).then_inc(gate_exp_done, 1)
            act.wait_ge(ld_expert, 64)
            for e in range(NE):
                for c in range(HC):
                    act.wait_ge(up_done, HC * e + 2 * (c // 2) + 2)
                    if e >= 2 and c == 0:
                        act.wait_ge(down_done, e - 1)
                    act.activation(hid[:, e % 2, c, :],
                                   ps_s[2 * (e % 2) + c // 2][:, CAP * (c % 2):CAP * (c % 2) + CAP],
                                   ACT.Gelu_apprx_tanh, bias=b1_sb[:, e, c:c + 1]).then_inc(gelu_done, 1)

        @block.tensor
        def _(pe):
            pe.wait_ge(prep_act, 2 * SPT)
            pe.wait_ge(prep_dve, 15)
            for a in range(2):
                for j in range(SLABS * 2):
                    mm = pe.matmul(ps_kv[:, a * E:a * E + E], bv_wide[:, a, j, :], wo_blk[:, a, 0, j, :],
                                   start=(a == 0 and j == 0), stop=True, skip_group_check=True)
            mm.then_inc(prep_pe, 1)
            pe.wait_ge(prep_dve, 17)

            def scores(n):
                wait(pe, qbf_done, n, 1, 1)
                wait(pe, kbf_done, n, 2, 2)
                for g in range(GROUPS):
                    wait(pe, exp_done, n, GROUPS, -GROUPS + g + 1)
                    rows = slice(32 * g, 32 * g + 32)
                    for s in range(SLABS):
                        for b in range(SPT):
                            mm = pe.matmul(ps_s[g][S * b:S * b + S, 2 * S * s:2 * S * s + 2 * S],
                                           q_bf[rows, n.par, s, S * b:S * b + S], k_blk_bf[rows, s, b],
                                           start=(s == 0), stop=True, skip_group_check=True)
                    mm.then_inc(s_done, 1)

            def project(n):
                wait(pe, turned_copied, n, 1, 1)
                kv, qs = turned[:, n.par, n.layer, :], turned[:, n.par, 0, :]
                for s in range(SLABS):
                    pe.matmul(ps_q[n.par][:, 128 * s:128 * s + 128],
                              wq_sb[:, n.layer, 128 * s:128 * s + 128], qs,
                              start=(s == 0), stop=False, skip_group_check=True)
                wait(pe, kt_done, n, SLABS, 0)
                wait(pe, v_done, n, 2, 0)
                for s in range(SLABS):
                    pe.matmul(ps_kv[:, 128 * s:128 * s + 128],
                              wk_sb[:, n.layer, 128 * s:128 * s + 128], kv,
                              start=(s == 0), stop=True, skip_group_check=True)
                mm = pe.matmul(ps_kv[:, SLABS * 128:SLABS * 128 + E], kv, wv_sb[:, n.layer, :],
                               start=False, stop=True, skip_group_check=True)
                mm.then_inc(proj_done, 1)

            def inject_max(n):
                wait(pe, max_done, n, GROUPS, GROUPS)
                for s in range(SLABS):
                    mm = pe.matmul(ps_q[n.par][:, 128 * s:128 * s + 128],
                                   neg_max[:, 8 * s:8 * s + 8, :], ident_bf[:],
                                   start=False, stop=True, skip_group_check=True)
                mm.then_inc(inject_done, 1)

            def attend(n):
                wait(pe, exp_done, n, GROUPS, GROUPS)
                wait(pe, v_done, n, 2, 2)
                wait(pe, resid_done, n, 1, 0)
                for j in range(SLABS * 2):
                    for g in range(GROUPS):
                        head = 8 * (j // 2) + 2 * g + j % 2
                        pe.matmul(ps_m[32 * g:32 * g + 32, S * j:S * j + S], v_blk[:, n.par, head],
                                  probs[:, n.par, g, j, :], start=(j == 0), stop=True,
                                  skip_group_check=True)
                for g in range(GROUPS):
                    mm = pe.matmul(ps_m[32 * g:32 * g + 32, 256:512], key_ones[:],
                                   probs[:, n.par, g], start=False, stop=True, skip_group_check=True)
                mm.then_inc(av_done, 1)

            def scores_turned(n):
                wait(pe, qblk_done, n, 2, 2)
                for g in range(GROUPS):
                    rows = slice(32 * g, 32 * g + 32)
                    for s in range(SLABS):
                        for b in range(SPT):
                            mm = pe.matmul(ps_s[g][S * b:S * b + S, 2 * S * s:2 * S * s + 2 * S],
                                           k_t[rows, n.par, s, S * b:S * b + S], q_blk[rows, s, b],
                                           start=(s == 0), stop=True, skip_group_check=True)
                    mm.then_inc(st_done, 1)

            def turns(n):
                wait(pe, qblk_done, n, 2, -2)
                wait(pe, xn_done, n, 1, 1)
                mm = pe.transpose(ps_q[n.par][:, 256:384], xn[:, n.par, :], ident[:])
                if n.layer:
                    c = Unit(n.number - T, n.pair)
                    if c.pair is None:
                        pe.wait_ge(ld_ctx[c.par], 16 * (c.number // 2 + 1))
                    else:
                        pe.wait_ge(ld_ctx[c.par], c.pair * 16 + 16 * (c.number // 2 + 1))
                    mm = pe.transpose(ps_q[n.par][:, 384:512], ctx_ring[:, n.par, :], ident[:])
                mm.then_inc(turns_done, 1)

            def project_out(n):
                wait(pe, attn_done, n, 1, 1)
                for j in range(SLABS * 2):
                    for b in range(SPT):
                        mm = pe.matmul(ps_m[S * b:S * b + S, 0:E], attn_t[:, n.par, j, :],
                                       wo_blk[:, n.layer, b, j, :], start=(j == 0),
                                       stop=(j == SLABS * 2 - 1), skip_group_check=True)
                mm.then_inc(y_done, 1)

            def step(n):
                if n.exists:
                    scores(n)
                if n.at(-2).exists:
                    project_out(n.at(-2))
                if n.at(1).exists:
                    project(n.at(1))
                if n.exists:
                    inject_max(n)
                if n.at(-1).exists:
                    attend(n.at(-1))
                if n.exists:
                    scores_turned(n)
                if n.at(2).exists:
                    turns(n.at(2))

            run_steps(pe, step)

            pe.wait_ge(exp_done, GROUPS * UNITS)
            for q in range(4):
                for t in range(4 * q, 4 * q + 4):
                    pe.wait_ge(xn3_done, t + 1)
                    mm = pe.transpose(ps_s[q][:, 128 * (t % 4):128 * (t % 4) + 128], xn3[:, t, :], ident[:])
                mm.then_inc(turns3_done, 1)
            pe.wait_ge(qblk_done, 2 * UNITS)
            pe.wait_ge(xt3_done, 4)
            pe.wait_ge(ld_gate, 64)
            for t in range(T):
                mm = pe.matmul(ps_q[0][:, NE * t:NE * t + NE], xt3[:, t, :], wg_sb[:], start=(t == 0), stop=True,
                               skip_group_check=True)
            mm.then_inc(logits_done, 1)
            pe.wait_ge(z_zero, 2)
            pe.wait_ge(gate_prep, 2)
            pe.wait_ge(total_done, 1)
            pe.matmul(ps_kv[:, 0:NE], ones_bf[:], first_count_bf[:], start=True, stop=True)
            pe.wait_ge(total_done, 2)
            for k in range(TOP):
                lo = k * T * NE
                pe.matmul(ps_q[1][:, lo:lo + T * NE], tri_bf[:], chosen[:, k].rearrange("p t e -> p (t e)"),
                          start=(k == 0), stop=False, skip_group_check=True)
                for t in range(T - 1):
                    mm = pe.matmul(ps_q[1][:, lo + NE * (t + 1):lo + NE * T], ones_bf[:],
                                   chosen[:, k, t:t + 1, :].to_broadcast([128, T - 1 - t, NE]),
                                   start=False, stop=(t == T - 2), skip_group_check=True)
            mm.then_inc(queue_done, 1)
            pe.wait_ge(facts_done, 4)
            for i in range(KT):
                pe.wait_ge(facts_done, 4 + i + 1)
                mm = pe.matmul(ps_m[:, 0:4 * BLOCKS], at_row[:, i, :], facts[:, i].rearrange("p v i -> p (v i)"),
                               start=(i == 0), stop=(i == KT - 1))
            mm.then_inc(table_done, 1)
            pe.wait_ge(ld_expert, 64)
            pe.wait_ge(rows_done, 2)

            def turn_tokens(e):
                if e >= 2:
                    pe.wait_ge(xet_done, e - 1)
                for i in range(2):
                    pe.wait_ge(gathered[2 * e + i], 16)
                    mm = pe.transpose(ps_x[e % 2][:, 128 * i:128 * i + 128], xe[:, 2 * e + i, :], ident[:])
                mm.then_inc(xe_turned, 1)

            def up(e):
                pe.wait_ge(xet_done, e + 1)
                for c in range(HC):
                    if e >= 2:
                        pe.wait_ge(gelu_done, HC * (e - 2) + 2 * (c // 2) + 2)
                    pe.matmul(ps_s[2 * (e % 2) + c // 2][:, CAP * (c % 2):CAP * (c % 2) + CAP],
                              w1_sb[:, e, 128 * c:128 * c + 128], xe_t[:, e, :], start=(c % 2 == 0), stop=True,
                              skip_group_check=True).then_inc(up_done, 1)

            def down(e):
                if e >= 2:
                    pe.wait_ge(ye_done, e - 1)
                for i in range(2):
                    for c in range(HC):
                        pe.wait_ge(gelu_done, HC * e + c + 1)
                        mm = pe.matmul(ps_y[e % 2][:, E * i:E * i + E], hid[:, e % 2, c, 128 * i:128 * i + 128],
                                       w2_sb[:, e, c, :], start=(i == 0 and c == 0), stop=(c == HC - 1),
                                       skip_group_check=True)
                mm.then_inc(down_done, 1)

            turn_tokens(0)
            for e in range(NE + 1):
                if e + 1 < NE:
                    turn_tokens(e + 1)
                if e < NE:
                    up(e)
                if e >= 1:
                    down(e - 1)


def kernel(**inputs):
    import numpy as np
    import concourse.bacc as bacc
    from concourse.bass_utils import run_bass_kernel_spmd

    def padded(a):
        a = np.asarray(a)
        wide = np.zeros(a.shape[:-1] + (H, SLOT), a.dtype)
        wide[..., 0:D] = a.reshape(a.shape[:-1] + (H, D))
        return wide.reshape(a.shape[:-1] + (H * SLOT,))

    def both(name, turn=False):
        a, b = np.asarray(inputs["L0_attn_" + name]), np.asarray(inputs["L0_xattn_" + name])
        return np.stack([a, b.T if turn else b])

    def columns(a):
        return np.ascontiguousarray(a.reshape(2, -1, 128).transpose(2, 0, 1))

    def by_group(a):
        n = a.shape[-1]
        wide = np.zeros((GROUPS, SPT, SLOT, 2, SLABS * 2, n), a.dtype)
        src = a.reshape(2, SLABS, GROUPS, 2, D, n).transpose(2, 4, 0, 1, 3, 5)
        wide[:, :, 0:D] = src.reshape(GROUPS, 1, D, 2, SLABS * 2, n)
        return wide.reshape(128, 2, SLABS * 2, n)

    row = np.arange(128)
    arrays = {
        "x_in": np.ascontiguousarray(np.asarray(inputs["x"]).reshape(NSEQ * S, E)),
        "ctx_in": np.ascontiguousarray(np.asarray(inputs["ctx_1024"]).reshape(NSEQ * S, E)),
        "wq": padded(both("Wq", True)), "wk": padded(both("Wk", True)),
        "wv": both("Wv", True), "wo": by_group(both("Wo", True)),
        "bq": columns(padded(both("bq"))), "bk": columns(padded(both("bk"))),
        "bv": by_group(both("bv")[..., None])[..., 0], "bo": both("bo"),
        "ident_in": np.eye(128, dtype=np.float32),
        "hmask_in": np.stack([row // SLOT % 2 == 0, row // SLOT % 2 == 1], 1).astype(np.float32),
        "kone_in": (row % SLOT == D).astype(np.float32).reshape(128, 1),
        "smask_in": np.stack([row // SLOT % 2 == b for b in range(SPT)], 1).astype(np.float32),
    }
    at = np.arange(KT)
    small = np.concatenate([NE - np.arange(NE), np.arange(NE), np.arange(BLOCKS), at % T, at // T])
    arrays["consts_in"] = np.concatenate([
        (row[:, None] <= row[None, :]), np.broadcast_to(row + 1, (128, 128)),
        np.broadcast_to(small, (128, small.size)), row[:, None]], 1).astype(np.float32)
    arrays["wg"] = np.asarray(inputs["L0_ffn_Wg"])
    arrays["w1"] = np.asarray(inputs["L0_ffn_W1"])
    arrays["b1"] = np.ascontiguousarray(np.asarray(inputs["L0_ffn_b1"]).reshape(NE, HC, 128).transpose(2, 0, 1))
    arrays["w2"] = np.asarray(inputs["L0_ffn_W2"])
    arrays["b2"] = np.asarray(inputs["L0_ffn_b2"])
    nc = bacc.Bacc("TRN2", target_bir_lowering=False, num_devices=1)
    args = [nc.dram_tensor(n, a.shape, mybir.dt.from_np(a.dtype), kind="ExternalInput").ap()
            for n, a in arrays.items()]
    out = nc.dram_tensor("out", (NSEQ * S, E), F32, kind="ExternalOutput").ap()
    decoder_layer(nc, *args, out)
    r = run_bass_kernel_spmd(nc, [arrays], core_ids=[0])
    return r.results[0]["out"].reshape(NSEQ, S, E)
```

```python
import concourse.bass as bass
from concourse import mybir
from contextlib import ExitStack

F32 = mybir.dt.float32
BF16 = mybir.dt.bfloat16
I32 = mybir.dt.int32
U32 = mybir.dt.uint32
ALU = mybir.AluOpType
ACT = mybir.ActivationFunctionType
AX = mybir.AxisListType

NSEQ, S, E = 32, 64, 128
H, D = 16, 8
T = NSEQ * S // 128
SPT = 128 // S
UNITS = 2 * T
PAIRS = H // 2
SLOT = 16
SLABS = H * SLOT // 128
GROUPS = 4
EPS = 1e-5
NE, TOP, HID = 8, 2, 512
WARM = [16, 2, 0, 4, 4, 4]
CAP = 256
HC = HID // 128
BLOCKS = NE * CAP // 128
KT = TOP * T
SCALE = 1.0 / float(D) ** 0.5


def decoder_layer(nc, x_in, ctx_in, weights, columns_in, bo, consts_in, wg, w1, b1, w2, b2, out):
    ctx = ExitStack()
    with ctx:
        def sb(name, shape, dt=F32):
            return ctx.enter_context(nc.sbuf_tensor(name, shape, dt))

        def bank(name):
            return ctx.enter_context(nc.psum_tensor(name, [128, 512], F32))

        def sem(name):
            return ctx.enter_context(nc.semaphore(name))

        x = sb("x", [128, T // 2, 2, E])
        ctx_ring = sb("ctx_ring", [128, 2, E])
        ident_bf = sb("ident_bf", [128, 128], BF16)
        WIDE = SLABS * 128
        w_sb = sb("w_sb", [128, 2, 2 * WIDE + 2 * E])
        wq_sb, wk_sb = w_sb[:, :, 0:WIDE], w_sb[:, :, WIDE:2 * WIDE]
        wv_sb, wo_sb = w_sb[:, :, 2 * WIDE:2 * WIDE + E], w_sb[:, :, 2 * WIDE + E:]
        columns_sb = sb("columns_sb", [128, 128 + 3 + 4 * SLABS + 2])
        ident = columns_sb[:, 0:128]
        hmask = columns_sb[:, 128:130]
        kone = columns_sb[:, 130:131]
        bq_sb = columns_sb[:, 131:131 + 2 * SLABS].rearrange("p (a s) -> p a s", a=2)
        bk_in = columns_sb[:, 131 + 2 * SLABS:131 + 4 * SLABS].rearrange("p (a s) -> p a s", a=2)
        bv_col = columns_sb[:, 131 + 4 * SLABS:]
        bk_sb = sb("bk_sb", [128, 2, SLABS])
        bq_masked = sb("bq_masked", [128, 2, 2, SLABS, SPT])
        bv_wide = sb("bv_wide", [128, 2, 128])
        bo_rows = sb("bo_rows", [128, 2, E])
        stats = sb("stats", [128, 6])
        meanvar = sb("meanvar", [128, 2, 2])
        logvar = sb("logvar", [128, 2, 1])
        eps_col = sb("eps_col", [128, 1])
        rstd = sb("rstd", [128, 2, 1])
        newton = sb("newton", [128, 2, 5])
        minus_half = sb("minus_half", [128, 1])
        three = sb("three", [128, 1])
        xn = sb("xn", [128, 2, E])
        turned = sb("turned", [128, 2, 2, 128])
        q_bf = sb("q_bf", [128, 2, SLABS, 128], BF16)
        q_blk = sb("q_blk", [128, SLABS, SPT, 2, S])
        k_t = sb("k_t", [128, 2, SLABS, 128])
        k_blk_bf = sb("k_blk_bf", [128, SLABS, SPT, 2, S], BF16)
        v_blk = sb("v_blk", [128, 2, H, SPT, SLOT])
        neg_max = sb("neg_max", [128, H, SLOT], BF16)
        probs = sb("probs", [128, 2, GROUPS, SLABS * 2, S])
        attended_sb = sb("attended_sb", [128, SLABS * 2 * S])
        inv_den = sb("inv_den", [128, SPT, PAIRS])
        attn = sb("attn", [128, 2, SPT, PAIRS, D])
        attn_t = sb("attn_t", [128, 2, 128])

        tri = sb("tri", [128, 128])
        tri_bf = sb("tri_bf", [128, 128], BF16)
        count_row = sb("count_row", [128, 128])
        count_bf = sb("count_bf", [128, 128], BF16)
        small = sb("small", [128, 2 * NE + BLOCKS + 2 * KT + 1])
        rank = small[:, 0:NE]
        expert_no = small[:, NE:2 * NE]
        block_no = small[:, 2 * NE:2 * NE + BLOCKS]
        tile_no = small[:, 2 * NE + BLOCKS:2 * NE + BLOCKS + KT]
        choice_no = small[:, 2 * NE + BLOCKS + KT:2 * NE + BLOCKS + 2 * KT]
        part_no = small[:, 2 * NE + BLOCKS + 2 * KT:]
        ones_bf = sb("ones_bf", [128, 128], BF16)
        wg_sb = sb("wg_sb", [128, NE])
        w1_sb = sb("w1_sb", [128, NE, HID])
        b1_sb = sb("b1_sb", [128, NE, HC])
        w2_sb = sb("w2_sb", [128, NE, HC, E])
        b2_rows = sb("b2_rows", [128, NE, E])
        zeros = sb("zeros", [128, 1024])
        stats3 = sb("stats3", [128, T, 6])
        meanvar3 = sb("meanvar3", [128, T, 2])
        rstd3 = sb("rstd3", [128, 5, T])
        xn3 = sb("xn3", [128, T, E])
        xt3 = sb("xt3", [128, T, 128])
        gate = sb("gate", [128, T, NE])
        gate_tmp = sb("gate_tmp", [128, T, NE])
        gate_col = sb("gate_col", [128, 4, T])
        best = sb("best", [128, TOP, T])
        chosen = sb("chosen", [128, TOP, T, NE], BF16)
        first_count = sb("first_count", [128, NE])
        first_count_bf = sb("first_count_bf", [128, NE], BF16)
        base = sb("base", [128, TOP, NE])
        order = sb("order", [128, TOP, T, NE])
        order_tmp = sb("order_tmp", [128, TOP, T, NE])
        place = sb("place", [128, KT])
        expert = sb("expert", [128, KT])
        upper = sb("upper", [128, KT])
        row_in = sb("row_in", [128, KT])
        blk = sb("blk", [128, KT])
        dropped = sb("dropped", [128, KT])
        kept = sb("kept", [128, KT])
        in_block = sb("in_block", [128, KT, BLOCKS])
        at_row = sb("at_row", [128, KT, 128], BF16)
        facts = sb("facts", [128, KT, 4, BLOCKS], BF16)
        table = sb("table", [128, 4, BLOCKS])
        src_f = sb("src_f", [128, BLOCKS])
        dst_f = sb("dst_f", [128, BLOCKS])
        src_row = sb("src_row", [128, BLOCKS], U32)
        dst_row = sb("dst_row", [128, BLOCKS], U32)
        xe = sb("xe", [128, BLOCKS, E])
        xe_t = sb("xe_t", [128, NE, CAP])
        hid = sb("hid", [128, 2, HC, CAP])
        ye = sb("ye", [128, BLOCKS, E])
        z = sb("z", [128, TOP, T, E])
        xn_rows = nc.dram_tensor("xn_rows", (NSEQ * S, E), F32).ap()
        z_rows = nc.dram_tensor("z_rows", (TOP * NSEQ * S, E), F32).ap()

        ps_q = [bank("ps_q0"), bank("ps_q1")]
        ps_kv = bank("ps_kv")
        ps_s = [bank("ps_s%d" % g) for g in range(GROUPS)]
        ps_m = bank("ps_m")
        attended = ps_m[:, 0:SLABS * 2 * S]
        attended_t = ps_m[:, 256:512].rearrange(
            "p (i b c) -> p i b c", b=SPT, c=SLOT)
        attn_turned_ps = ps_m[:, 0:128]
        y_ps = ps_kv[:, 384:384 + E]

        ld_const = sem("ld_const")
        ld_w = sem("ld_w")
        ld_x = [sem("ld_x%d" % i) for i in range(4)]
        ld_ctx = [sem("ld_ctx0"), sem("ld_ctx1")]
        st_out = sem("st_out")
        prep_pool = sem("prep_pool")
        prep_dve = sem("prep_dve")
        prep_pe = sem("prep_pe")
        bias_added = sem("bias_added")
        stats_done = sem("stats_done")
        aggr_done = sem("aggr_done")
        logvar_done = sem("logvar_done")
        rstd0_done = sem("rstd0_done")
        newton_done = sem("newton_done")
        xn_done = sem("xn_done")
        turns_done = sem("turns_done")
        turned_copied = sem("turned_copied")
        projq_done = sem("projq_done")
        proj_done = sem("proj_done")
        kt_done = sem("kt_done")
        qbf_done = sem("qbf_done")
        kbf_done = sem("kbf_done")
        v_done = sem("v_done")
        s_done = sem("s_done")
        max_done = sem("max_done")
        inject_done = sem("inject_done")
        qblk_done = sem("qblk_done")
        st_done = sem("st_done")
        exp_done = sem("exp_done")
        av_done = sem("av_done")
        av_copied = sem("av_copied")
        av_turned = sem("av_turned")
        inv_done = sem("inv_done")
        attn_done = sem("attn_done")
        attn_turned = sem("attn_turned")
        attnt_done = sem("attnt_done")
        y_done = sem("y_done")
        resid_done = sem("resid_done")

        ld_gate = sem("ld_gate")
        gate_prep = sem("gate_prep")
        ld_expert = sem("ld_expert")
        z_zero = sem("z_zero")
        z_cleared = sem("z_cleared")
        st_xn = sem("st_xn")
        gathered = [sem("gathered%d" % i) for i in range(BLOCKS)]
        st_z = sem("st_z")
        ld_z = [sem("ld_z%d" % i) for i in range(4)]
        stats3_done = sem("stats3_done")
        rstd3_done = sem("rstd3_done")
        newton3_done = sem("newton3_done")
        xn3_done = sem("xn3_done")
        turns3_done = sem("turns3_done")
        xt3_done = sem("xt3_done")
        logits_done = sem("logits_done")
        shifted_done = sem("shifted_done")
        gate_exp_done = sem("gate_exp_done")
        route = sem("route")
        total_done = sem("total_done")
        queue_done = sem("queue_done")
        facts_done = sem("facts_done")
        table_done = sem("table_done")
        rows_done = sem("rows_done")
        xe_turned = sem("xe_turned")
        xet_done = sem("xet_done")
        up_done = sem("up_done")
        gelu_done = sem("gelu_done")
        down_done = sem("down_done")
        ye_done = sem("ye_done")
        out_done = sem("out_done")

        block = ctx.enter_context(nc.Block())
        ps_x = [ps_kv, ps_m]
        ps_y = ps_q

        class Unit:

            def __init__(self, number, pair=None):
                self.number, self.pair = number, pair
                self.par = number % 2
                self.layer = number // T

            def at(self, k):
                return Unit(self.number + k, self.pair)

            @property
            def exists(self):
                return 0 <= self.number < UNITS

            def tile_pair(self):
                p = (self.number % T) // 2
                return p if self.pair is None else self.pair + p

            def x(self):
                return x[:, self.tile_pair(), self.par, :]

            def count(self, per, extra=0):
                n = per * self.number + extra
                return n if self.pair is None else self.pair * (2 * per) + n

        def wait(eng, semaphore, unit, per, extra=0):
            if unit.pair is None:
                if unit.count(per, extra) > 0:
                    eng.wait_ge(semaphore, unit.count(per, extra))
            else:
                eng.wait_ge(semaphore, unit.count(per, extra))

        FIRST, LAST = -3, UNITS + 1
        LOOP_FROM, LOOP_STEPS = 2, 10

        def run_steps(eng, step):
            n = FIRST
            while n <= LAST:
                if n % T == LOOP_FROM and 0 <= n < UNITS:
                    with eng.Fori(0, LOOP_STEPS // 2) as pair:
                        for k in range(2):
                            step(Unit(n + k, pair))
                    n += LOOP_STEPS
                else:
                    step(Unit(n))
                    n += 1

        @block.sync
        def _(sp):
            x_tiles = x_in.rearrange("(i k p) e -> p i k e", k=2, p=128)
            ctx_tiles = ctx_in.rearrange("(i k p) e -> p i k e", k=2, p=128)
            for q in range(4):
                sp.dma_start(x[:, 2 * q:2 * q + 2], x_tiles[:, 2 * q:2 * q + 2]).then_inc(ld_x[q], 16)

            sp.wait_ge(ld_w, 48)
            sp.wait_ge(ld_x[3], 16)
            sp.dma_start(wg_sb[:], wg).then_inc(ld_gate, 16)
            sp.dma_start(tri[:], consts_in[:, 0:128]).then_inc(ld_gate, 16)
            sp.dma_start(count_row[:], consts_in[:, 128:256]).then_inc(ld_gate, 16)
            sp.dma_start(small[:], consts_in[:, 256:]).then_inc(ld_gate, 16)
            sp.dma_start(b1_sb[:], b1).then_inc(ld_expert, 16)
            sp.dma_start(b2_rows[:], b2.rearrange("(q x) e -> q x e", q=1).to_broadcast([128, NE, E]))\
              .then_inc(ld_expert, 16)
            sp.dma_start(w1_sb[:], w1.rearrange("x d h -> d x h")).then_inc(ld_expert, 16)
            sp.dma_start(w2_sb[:], w2.rearrange("x (c p) e -> p x c e", p=128)).then_inc(ld_expert, 16)
            sp.wait_ge(z_zero, 1)
            z_flat = z_rows.rearrange("(c p r) e -> c p (r e)", p=128, r=8)
            for c in range(TOP * NSEQ * S // 1024):
                sp.dma_start(z_flat[c], zeros[:]).then_inc(z_cleared, 16)

            def load_ctx(u):
                wait(sp, turns_done, u, 1, -1)
                sp.dma_start(ctx_ring[:, u.par, :], ctx_tiles[:, u.tile_pair(), u.par, :])\
                  .then_inc(ld_ctx[u.par], 16)

            for t in range(2):
                load_ctx(Unit(T + t))
            with sp.Fori(0, T // 2 - 1) as pair:
                for k in range(2):
                    load_ctx(Unit(T + 2 + k, pair))
            xn_tiles = xn_rows.rearrange("(t p) e -> p t e", p=128)
            for q in range(4):
                sp.wait_ge(xn3_done, 4 * q + 4)
                sp.dma_start(xn_tiles[:, 4 * q:4 * q + 4], xn3[:, 4 * q:4 * q + 4]).then_inc(st_xn, 16)
            z_tiles = z_rows.rearrange("(k t p) e -> p k t e", k=TOP, p=128)
            sp.wait_ge(st_z, 16 * BLOCKS)
            for q in range(4):
                tiles = slice(4 * q, 4 * q + 4)
                for k in range(TOP):
                    sp.dma_start(z[:, k, tiles], z_tiles[:, k, tiles]).then_inc(ld_z[q], 16)
            out_tiles = out.rearrange("(i k p) e -> p i k e", k=2, p=128)
            for q in range(4):
                sp.wait_ge(out_done, 8 * q + 8)
                sp.dma_start(out_tiles[:, 2 * q:2 * q + 2], x[:, 2 * q:2 * q + 2]).then_inc(st_out, 16)
            sp.wait_ge(st_out, 64)

        @block.gpsimd
        def _(pool):
            nc.gpsimd.memset(zeros[:], 0.0).then_inc(z_zero, 1)
            nc.gpsimd.memset(ones_bf[:], 1.0).then_inc(z_zero, 1)
            nc.gpsimd.memset(v_blk[:], 0.0).then_inc(prep_pool, 1)
            nc.gpsimd.memset(neg_max[:], 0.0).then_inc(prep_pool, 1)
            nc.gpsimd.memset(eps_col[:], EPS).then_inc(prep_pool, 1)
            nc.gpsimd.memset(minus_half[:], -0.5).then_inc(prep_pool, 1)
            nc.gpsimd.memset(three[:], 3.0).then_inc(prep_pool, 1)
            for b in range(SPT):
                pool.wait_ge(prep_pool, 5 + b)
                nc.gpsimd.memset(v_blk[S * b:S * b + S, :, :, b, D], 1.0).then_inc(prep_pool, 1)
            pool.wait_ge(prep_pool, 7)

            def step(n):
                u, old = n.at(3), n.at(2)
                if u.exists:
                    v, yy, vyy, less3, half = (newton[:, u.par, i:i + 1] for i in range(5))
                    y = rstd[:, u.par, :]
                    wait(pool, rstd0_done, u, 1, 1)
                    nc.gpsimd.tensor_tensor(v, meanvar[:, u.par, 1:2], eps_col[:], ALU.add)\
                      .then_inc(newton_done, 1)
                    nc.gpsimd.tensor_tensor(yy, y, y, ALU.mult).then_inc(newton_done, 1)
                    nc.gpsimd.tensor_tensor(half, y, minus_half[:], ALU.mult).then_inc(newton_done, 1)
                    wait(pool, newton_done, u, 6, 3)
                    nc.gpsimd.tensor_tensor(vyy, yy, v, ALU.mult).then_inc(newton_done, 1)
                    wait(pool, newton_done, u, 6, 4)
                    nc.gpsimd.tensor_tensor(less3, vyy, three[:], ALU.subtract).then_inc(newton_done, 1)
                    wait(pool, newton_done, u, 6, 5)
                    nc.gpsimd.tensor_tensor(y, less3, half, ALU.mult).then_inc(newton_done, 1)
                if old.exists:
                    wait(pool, xn_done, old, 1, 1)
                    nc.gpsimd.tensor_tensor(old.x(), old.x(), bo_rows[:, old.layer, :], ALU.add)\
                      .then_inc(bias_added, 1)

            run_steps(pool, step)

            v, t0, t1, y, y1 = (rstd3[:, i, :] for i in range(5))
            pool.wait_ge(rstd3_done, 2)
            nc.gpsimd.tensor_scalar(v, meanvar3[:, :, 1], EPS, None, ALU.add).then_inc(newton3_done, 1)
            nc.gpsimd.tensor_tensor(t0, y, y, ALU.mult).then_inc(newton3_done, 1)
            pool.wait_ge(newton3_done, 2)
            nc.gpsimd.tensor_tensor(t0, t0, v, ALU.mult).then_inc(newton3_done, 1)
            pool.wait_ge(newton3_done, 3)
            nc.gpsimd.tensor_scalar(t1, t0, -0.5, 1.5, ALU.mult, ALU.add).then_inc(newton3_done, 1)
            pool.wait_ge(newton3_done, 4)
            nc.gpsimd.tensor_tensor(y1, y, t1, ALU.mult).then_inc(newton3_done, 1)
            pool.wait_ge(rows_done, 2)
            pool.wait_ge(st_xn, 64)
            for i in range(BLOCKS):
                pool.indirect_dma_start(out=xe[:, i, :], out_offset=None, in_=xn_rows,
                                        in_offset=bass.IndirectOffsetOnAxis(ap=src_row[:, i:i + 1], axis=0))\
                    .then_inc(gathered[i], 16)
            pool.wait_ge(z_cleared, 16 * (TOP * NSEQ * S // 1024))
            for i in range(BLOCKS):
                pool.wait_ge(ye_done, i // 2 + 1)
                pool.indirect_dma_start(out=z_rows,
                                        out_offset=bass.IndirectOffsetOnAxis(ap=dst_row[:, i:i + 1], axis=0),
                                        in_=ye[:, i, :], in_offset=None,
                                        bounds_check=TOP * NSEQ * S - 1, oob_is_err=False)\
                    .then_inc(st_z, 16)

        @block.vector
        def _(dve):
            dve.wait_ge(ld_const, 16)
            nc.vector.tensor_copy(ident_bf[:], ident[:]).then_inc(prep_dve, 1)
            for a in range(2):
                nc.vector.tensor_scalar(bk_sb[:, a, :], bk_in[:, a, :], kone[:, 0:1], None, ALU.add)\
                  .then_inc(prep_dve, 1)
                nc.vector.tensor_copy(bv_wide[:, a, :], bv_col[:, a:a + 1].to_broadcast([128, 128]))\
                  .then_inc(prep_dve, 1)
                for hh in range(2):
                    nc.vector.tensor_scalar(bq_masked[:, a, hh],
                                            bq_sb[:, a, :].unsqueeze(2).to_broadcast([128, SLABS, SPT]),
                                            hmask[:, hh:hh + 1], None, ALU.mult).then_inc(prep_dve, 1)
            dve.wait_ge(prep_pe, 1)
            dve.wait_ge(ld_w, 48)
            for a in range(2):
                nc.vector.tensor_tensor(bo_rows[:, a, :], bo_rows[:, a, :],
                                        ps_kv[:, a * E:a * E + E], ALU.add).then_inc(prep_dve, 1)
            dve.wait_ge(prep_dve, 11)

            def step(n):
                ln, nx2, nxt, prev, old = n.at(3), n.at(2), n.at(1), n.at(-1), n.at(-2)
                if ln.exists:
                    if ln.layer == 0:
                        if ln.pair is None:
                            dve.wait_ge(ld_x[ln.number // 4], 16)
                        else:
                            for q in ld_x:
                                dve.wait_ge(q, 16)
                    else:
                        wait(dve, resid_done, ln, 1, -T + 1)
                    wait(dve, aggr_done, ln, 1, 0)
                    nc.vector.bn_stats(stats[:], ln.x()).then_inc(stats_done, 1)
                    wait(dve, stats_done, ln, 1, 1)
                    wait(dve, xn_done, ln, 1, -1)

                def group_max(g):
                    wait(dve, s_done, n, GROUPS, g + 1)
                    nc.vector.tensor_reduce(
                        neg_max[:].rearrange("p (s g j) c -> p s g j c", s=SLABS, g=GROUPS)[:, :, g, :, D],
                        ps_s[g][:, 0:SLABS * 2 * S].rearrange("p (s j k) -> p s j k", s=SLABS, k=S),
                        AX.X, ALU.max, negate=True).then_inc(max_done, 1)

                if n.exists:
                    if n.number == 0:
                        dve.wait_ge(prep_pool, 7)
                    wait(dve, inject_done, n, 1, 0)
                    for g in range(GROUPS):
                        group_max(g)
                if ln.exists:
                    nc.vector.bn_aggr(meanvar[:, ln.par, :], stats[:]).then_inc(aggr_done, 1)
                if old.exists:
                    wait(dve, y_done, old, 1, 1)
                    wait(dve, bias_added, old, 1, 1)
                    nc.vector.tensor_tensor(old.x(), old.x(), y_ps, ALU.add)\
                      .then_inc(resid_done, 1)
                if n.exists:
                    wait(dve, inject_done, n, 1, 1)
                    for hh in range(2):
                        nc.vector.scalar_tensor_tensor(
                            out=q_blk[:, :, :, hh, :],
                            in0=ps_q[n.par][:, 0:SLABS * 128].rearrange("p (s b t) -> p s b t", s=SLABS, b=SPT),
                            scalar=hmask[:, hh:hh + 1],
                            in1=bq_masked[:, n.layer, hh].unsqueeze(3).to_broadcast([128, SLABS, SPT, S]),
                            op0=ALU.mult, op1=ALU.add).then_inc(qblk_done, 1)
                if prev.exists:
                    wait(dve, av_turned, prev, 1, 1)
                    nc.vector.reciprocal(inv_den[:], attended_t[:, :, :, D].rearrange("p i b -> p b i"))\
                      .then_inc(inv_done, 1)
                    wait(dve, inv_done, prev, 1, 1)
                    nc.vector.tensor_tensor(
                        attn[:, prev.par], attended_t[:, :, :, 0:D].rearrange("p i b d -> p b i d"),
                        inv_den[:].unsqueeze(3).to_broadcast([128, SPT, PAIRS, D]),
                        ALU.mult).then_inc(attn_done, 1)
                if nx2.exists:
                    wait(dve, newton_done, nx2, 6, 6)
                    wait(dve, turns_done, nx2, 1, -1)
                    nc.vector.tensor_scalar(xn[:, nx2.par, :], nx2.x(), meanvar[:, nx2.par, 0:1],
                                            rstd[:, nx2.par, :], ALU.subtract, ALU.mult).then_inc(xn_done, 1)
                if nxt.exists:
                    wait(dve, projq_done, nxt, SLABS, SLABS)
                    nc.vector.tensor_tensor(
                        q_bf[:, nxt.par], ps_q[nxt.par][:, 0:SLABS * 128].rearrange("p (s t) -> p s t", s=SLABS),
                        bq_sb[:, nxt.layer, :].unsqueeze(2).to_broadcast([128, SLABS, 128]),
                        ALU.add).then_inc(qbf_done, 1)
                    wait(dve, kt_done, nxt, SLABS, SLABS)
                    wait(dve, s_done, n, GROUPS, GROUPS)
                    for hh in range(2):
                        nc.vector.tensor_scalar(
                            k_blk_bf[:, :, :, hh, :],
                            k_t[:, nxt.par].rearrange("p s (b t) -> p s b t", b=SPT),
                            hmask[:, hh:hh + 1], None, ALU.mult).then_inc(kbf_done, 1)
            run_steps(dve, step)

            dve.wait_ge(ld_gate, 64)
            nc.vector.tensor_copy(tri_bf[:], tri[:]).then_inc(gate_prep, 1)
            nc.vector.tensor_copy(count_bf[:], count_row[:]).then_inc(gate_prep, 1)
            for t in range(T):
                dve.wait_ge(resid_done, T + t + 1)
                nc.vector.bn_stats(stats3[:, t, :], x[:, t // 2, t % 2, :]).then_inc(stats3_done, 1)
            for t in range(T):
                dve.wait_ge(stats3_done, t + 1)
                nc.vector.bn_aggr(meanvar3[:, t, :], stats3[:, t, :]).then_inc(stats3_done, 1)
            dve.wait_ge(newton3_done, 5)
            for t in range(T):
                nc.vector.tensor_scalar(xn3[:, t, :], x[:, t // 2, t % 2, :], meanvar3[:, t, 0:1],
                                        rstd3[:, 4, t:t + 1], ALU.subtract, ALU.mult).then_inc(xn3_done, 1)
            for q in range(2):
                dve.wait_ge(turns3_done, 2 * q + 2)
                nc.vector.tensor_copy(xt3[:, 8 * q + 4:8 * q + 8, :],
                                      ps_s[2 * q + 1][:].rearrange("p (t n) -> p t n", n=128))\
                    .then_inc(xt3_done, 1)

            steps = [0]

            def then(ins):
                steps[0] += 1
                ins.then_inc(route, 1)
                dve.wait_ge(route, steps[0])

            def wide(col):
                return col.unsqueeze(2).to_broadcast([128, T, NE])

            dve.wait_ge(logits_done, 1)
            logits = ps_q[0][:, 0:T * NE].rearrange("p (t e) -> p t e", e=NE)
            then(nc.vector.tensor_reduce(gate_col[:, 0], logits, AX.X, ALU.max))
            nc.vector.tensor_tensor(gate[:], logits, wide(gate_col[:, 0]), ALU.subtract)\
                .then_inc(shifted_done, 1)
            dve.wait_ge(gate_exp_done, 1)
            then(nc.vector.tensor_reduce(gate_col[:, 1], gate[:], AX.X, ALU.add))
            then(nc.vector.reciprocal(gate_col[:, 2], gate_col[:, 1]))
            then(nc.vector.tensor_tensor(gate[:], gate[:], wide(gate_col[:, 2]), ALU.mult))
            for k in range(TOP):
                then(nc.vector.tensor_reduce(best[:, k, :], gate[:], AX.X, ALU.max))
                then(nc.vector.tensor_tensor(gate_tmp[:], gate[:], wide(best[:, k, :]), ALU.is_equal))
                then(nc.vector.tensor_tensor(gate_tmp[:], gate_tmp[:],
                                             rank.unsqueeze(1).to_broadcast([128, T, NE]), ALU.mult))
                then(nc.vector.tensor_reduce(gate_col[:, 3], gate_tmp[:], AX.X, ALU.max))
                then(nc.vector.tensor_tensor(chosen[:, k], gate_tmp[:], wide(gate_col[:, 3]), ALU.is_equal))
                if k == 0:
                    then(nc.vector.scalar_tensor_tensor(out=gate[:], in0=chosen[:, 0], scalar=-2.0, in1=gate[:],
                                                        op0=ALU.mult, op1=ALU.add))
                    then(nc.vector.tensor_reduce(first_count[:], chosen[:, 0].rearrange("p t e -> p e t"),
                                                 AX.X, ALU.add))
                    nc.vector.tensor_copy(first_count_bf[:], first_count[:]).then_inc(total_done, 1)
                else:
                    nc.vector.tensor_copy(base[:, 0, :], zeros[:, 0:NE]).then_inc(total_done, 1)
            then(nc.vector.tensor_tensor(gate_col[:, 0], best[:, 0, :], best[:, 1, :], ALU.add))
            then(nc.vector.tensor_scalar(gate_col[:, 1], gate_col[:, 0], 1e-9, None, ALU.add))
            then(nc.vector.reciprocal(gate_col[:, 2], gate_col[:, 1]))
            then(nc.vector.tensor_tensor(best[:], best[:],
                                         gate_col[:, 2].unsqueeze(1).to_broadcast([128, TOP, T]), ALU.mult))
            then(nc.vector.tensor_tensor(order_tmp[:].rearrange("p k t e -> p (k t) e"),
                                         chosen[:].rearrange("p k t e -> p (k t) e"),
                                         expert_no.unsqueeze(1).to_broadcast([128, KT, NE]), ALU.mult))
            then(nc.vector.tensor_reduce(expert[:], order_tmp[:].rearrange("p k t e -> p (k t) e"), AX.X, ALU.add))
            dve.wait_ge(queue_done, 1)
            then(nc.vector.tensor_scalar(base[:, 1, :], ps_kv[:, 0:NE], float(CAP), None, ALU.min))
            then(nc.vector.tensor_tensor(order[:], ps_q[1][:, 0:KT * NE].rearrange("p (k t e) -> p k t e", t=T, e=NE),
                                         base[:].unsqueeze(2).to_broadcast([128, TOP, T, NE]), ALU.add))
            then(nc.vector.tensor_tensor(order[:], order[:], chosen[:], ALU.mult))
            then(nc.vector.tensor_reduce(place[:], order[:].rearrange("p k t e -> p (k t) e"), AX.X, ALU.add))
            then(nc.vector.tensor_scalar(upper[:], place[:], 128.5, None, ALU.is_gt))
            then(nc.vector.scalar_tensor_tensor(out=row_in[:], in0=upper[:], scalar=-128.0, in1=place[:],
                                                op0=ALU.mult, op1=ALU.add))
            then(nc.vector.tensor_scalar(dropped[:], place[:], CAP + 0.5, None, ALU.is_gt))
            then(nc.vector.scalar_tensor_tensor(out=blk[:], in0=expert[:], scalar=float(CAP // 128), in1=upper[:],
                                                op0=ALU.mult, op1=ALU.add))
            then(nc.vector.scalar_tensor_tensor(out=blk[:], in0=dropped[:], scalar=float(4 * BLOCKS), in1=blk[:],
                                                op0=ALU.mult, op1=ALU.add))
            then(nc.vector.tensor_scalar(kept[:], dropped[:], -1.0, 1.0, ALU.mult, ALU.add))
            then(nc.vector.tensor_tensor(best[:], best[:], kept[:].rearrange("p (k t) -> p k t", k=TOP), ALU.mult))
            then(nc.vector.tensor_tensor(in_block[:], block_no.unsqueeze(1).to_broadcast([128, KT, BLOCKS]),
                                         blk[:].unsqueeze(2).to_broadcast([128, KT, BLOCKS]), ALU.is_equal))
            nc.vector.tensor_scalar(facts[:, :, 0, :], in_block[:], part_no, None, ALU.mult)\
                .then_inc(facts_done, 1)
            nc.vector.tensor_tensor(facts[:, :, 1, :], in_block[:],
                                    tile_no.unsqueeze(2).to_broadcast([128, KT, BLOCKS]), ALU.mult)\
                .then_inc(facts_done, 1)
            nc.vector.tensor_tensor(facts[:, :, 2, :], in_block[:],
                                    choice_no.unsqueeze(2).to_broadcast([128, KT, BLOCKS]), ALU.mult)\
                .then_inc(facts_done, 1)
            nc.vector.tensor_copy(facts[:, :, 3, :], in_block[:]).then_inc(facts_done, 1)
            for i in range(KT):
                nc.vector.tensor_scalar(at_row[:, i, :], count_bf[:], row_in[:, i:i + 1], None, ALU.is_equal)\
                    .then_inc(facts_done, 1)
            dve.wait_ge(table_done, 1)
            then(nc.vector.tensor_copy(table[:], ps_m[:, 0:4 * BLOCKS].rearrange("p (v i) -> p v i", v=4)))
            then(nc.vector.scalar_tensor_tensor(out=src_f[:], in0=table[:, 1], scalar=128.0, in1=table[:, 0],
                                                op0=ALU.mult, op1=ALU.add))
            nc.vector.tensor_copy(src_row[:], src_f[:]).then_inc(rows_done, 1)
            then(nc.vector.tensor_scalar(dst_f[:], table[:, 3], -8192.0, 8192.0, ALU.mult, ALU.add))
            then(nc.vector.tensor_tensor(dst_f[:], dst_f[:], src_f[:], ALU.add))
            then(nc.vector.scalar_tensor_tensor(out=dst_f[:], in0=table[:, 2], scalar=float(NSEQ * S), in1=dst_f[:],
                                                op0=ALU.mult, op1=ALU.add))
            nc.vector.tensor_copy(dst_row[:], dst_f[:]).then_inc(rows_done, 1)

            def expert_tokens(e):
                dve.wait_ge(xe_turned, e + 1)
                nc.vector.tensor_copy(xe_t[:, e, :], ps_x[e % 2][:, 0:CAP]).then_inc(xet_done, 1)

            def expert_answer(e):
                dve.wait_ge(down_done, e + 1)
                nc.vector.tensor_tensor(ye[:, 2 * e:2 * e + 2, :],
                                        ps_y[e % 2][:, 0:2 * E].rearrange("p (i n) -> p i n", i=2),
                                        b2_rows[:, e:e + 1, :].to_broadcast([128, 2, E]), ALU.add)\
                    .then_inc(ye_done, 1)

            dve.wait_ge(ld_expert, 64)
            for e in range(NE + 2):
                if e < NE:
                    expert_tokens(e)
                if e >= 2:
                    expert_answer(e - 2)
            for q in range(4):
                dve.wait_ge(ld_z[q], 32)
                for k in range(TOP):
                    for t in range(4 * q, 4 * q + 4):
                        if k:
                            dve.wait_ge(out_done, 8 * q + t % 4 + 1)
                        row = x[:, t // 2, t % 2, :]
                        nc.vector.scalar_tensor_tensor(out=row, in0=z[:, k, t, :], scalar=best[:, k, t:t + 1],
                                                       in1=row, op0=ALU.mult, op1=ALU.add).then_inc(out_done, 1)

        @block.scalar
        def _(act):
            act.dma_start(columns_sb[:], columns_in).then_inc(ld_const, 16)
            act.dma_start(w_sb[:, 0], weights[:, 0]).then_inc(ld_w, 16)
            act.dma_start(w_sb[:, 1], weights[:, 1]).then_inc(ld_w, 16)
            act.dma_start(bo_rows[:], bo.rearrange("(q a) n -> q a n", q=1).to_broadcast([128, 2, E]))\
               .then_inc(ld_w, 16)

            act.preload_act_table_set("natural_log_exp_and_others")
            act.wait_ge(prep_pool, 7)

            def step(n):
                nxt, prev, ln = n.at(1), n.at(-1), n.at(3)
                if nxt.exists:
                    wait(act, turns_done, nxt, 1, 1)
                    wait(act, proj_done, nxt, 1, -1)
                    act.activation(turned[:, nxt.par, 0:1 + nxt.layer, :],
                                   ps_q[nxt.par][:, 256:256 + 128 * (1 + nxt.layer)].rearrange(
                                       "p (j t) -> p j t", t=128), ACT.Copy).then_inc(turned_copied, 1)
                if prev.exists:
                    wait(act, av_done, prev, 1, 1)
                    act.activation(attended_sb[:], attended, ACT.Copy).then_inc(av_copied, 1)

                def exponentials(g):
                    wait(act, st_done, n, GROUPS, g + 1)
                    act.activation(probs[:, n.par, g], ps_s[g][:, 0:SLABS * 2 * S].rearrange(
                        "p (j q) -> p j q", q=S), ACT.Exp, scale=SCALE).then_inc(exp_done, 1)

                if n.exists:
                    exponentials(0)
                if nxt.exists:
                    wait(act, proj_done, nxt, 1, 1)
                    wait(act, st_done, nxt, GROUPS, -GROUPS)
                    for s in range(SLABS):
                        act.activation(k_t[:, nxt.par, s, :], ps_kv[:, 128 * s:128 * s + 128],
                                       ACT.Identity, bias=bk_sb[:, nxt.layer, s:s + 1]).then_inc(kt_done, 1)
                if ln.exists:
                    wait(act, aggr_done, ln, 1, 1)
                    act.activation(logvar[:, ln.par, :], meanvar[:, ln.par, 1:2], ACT.Ln,
                                   bias=eps_col[:, 0:1]).then_inc(logvar_done, 1)
                if n.exists:
                    exponentials(1)
                if ln.exists:
                    wait(act, logvar_done, ln, 1, 1)
                    act.activation(rstd[:, ln.par, :], logvar[:, ln.par, :], ACT.Exp, scale=-0.5)\
                       .then_inc(rstd0_done, 1)
                if prev.exists:
                    wait(act, attn_turned, prev, 1, 1)
                    act.activation(attn_t[:, prev.par, :], attn_turned_ps, ACT.Copy).then_inc(attnt_done, 1)
                if nxt.exists:
                    wait(act, av_done, n, 1, 0)
                    for b in range(SPT):
                        rows = slice(S * b, S * b + S)
                        act.activation(v_blk[rows, nxt.par, :, b, 0:D],
                                       ps_kv[rows, SLABS * 128:SLABS * 128 + 128].rearrange(
                                           "p (h d) -> p h d", d=D), ACT.Copy).then_inc(v_done, 1)
                if n.exists:
                    exponentials(2)
                    exponentials(3)

            run_steps(act, step)

            act.wait_ge(stats3_done, 2 * T)
            act.activation(rstd3[:, 0, :], meanvar3[:, :, 1], ACT.Ln, bias=eps_col[:, 0:1]).then_inc(rstd3_done, 1)
            act.wait_ge(rstd3_done, 1)
            act.activation(rstd3[:, 3, :], rstd3[:, 0, :], ACT.Exp, scale=-0.5).then_inc(rstd3_done, 1)
            for q in range(2):
                act.wait_ge(turns3_done, 2 * q + 1)
                act.activation(xt3[:, 8 * q:8 * q + 4, :], ps_s[2 * q][:].rearrange("p (t n) -> p t n", n=128),
                               ACT.Copy).then_inc(xt3_done, 1)
            act.wait_ge(shifted_done, 1)
            act.activation(gate[:], gate[:], ACT.Exp).then_inc(gate_exp_done, 1)
            act.wait_ge(ld_expert, 64)
            for e in range(NE):
                for c in range(HC):
                    act.wait_ge(up_done, HC * e + 2 * (c // 2) + 2)
                    if e >= 2 and c == 0:
                        act.wait_ge(down_done, e - 1)
                    act.activation(hid[:, e % 2, c, :],
                                   ps_s[2 * (e % 2) + c // 2][:, CAP * (c % 2):CAP * (c % 2) + CAP],
                                   ACT.Gelu_apprx_tanh, bias=b1_sb[:, e, c:c + 1]).then_inc(gelu_done, 1)

        @block.tensor
        def _(pe):
            def warm(count):
                for _ in range(count):
                    pe.matmul(ps_m[:], ones_bf[:], zeros[:, 0:256].bitcast(BF16), start=True, stop=True)

            pe.wait_ge(z_zero, 2)
            warm(WARM[0])
            pe.wait_ge(prep_dve, 9)
            pe.wait_ge(ld_w, 48)
            warm(WARM[1])
            for a in range(2):
                mm = pe.matmul(ps_kv[:, a * E:a * E + E], bv_wide[:, a, :], wo_sb[:, a, :],
                               start=(a == 0), stop=True, skip_group_check=True)
            mm.then_inc(prep_pe, 1)
            pe.wait_ge(prep_dve, 11)

            def scores(n):
                wait(pe, qbf_done, n, 1, 1)
                wait(pe, kbf_done, n, 2, 2)
                for g in range(GROUPS):
                    wait(pe, exp_done, n, GROUPS, -GROUPS + g + 1)
                    rows = slice(32 * g, 32 * g + 32)
                    for s in range(SLABS):
                        for b in range(SPT):
                            mm = pe.matmul(ps_s[g][S * b:S * b + S, 2 * S * s:2 * S * s + 2 * S],
                                           q_bf[rows, n.par, s, S * b:S * b + S], k_blk_bf[rows, s, b],
                                           start=(s == 0), stop=True, skip_group_check=True)
                    mm.then_inc(s_done, 1)

            def project_q(n, s):
                if s == 0:
                    wait(pe, turned_copied, n, 1, 1)
                pe.matmul(ps_q[n.par][:, 128 * s:128 * s + 128],
                          wq_sb[:, n.layer, 128 * s:128 * s + 128], turned[:, n.par, 0, :],
                          start=(s == 0), stop=False, skip_group_check=True).then_inc(projq_done, 1)

            def project_k(n):
                wait(pe, resid_done, n, 1, -2)
                wait(pe, kt_done, n, SLABS, 0)
                wait(pe, v_done, n, 2, 0)
                for s in range(SLABS):
                    pe.matmul(ps_kv[:, 128 * s:128 * s + 128],
                              wk_sb[:, n.layer, 128 * s:128 * s + 128], turned[:, n.par, n.layer, :],
                              start=(s == 0), stop=True, skip_group_check=True)

            def project_v(n):
                mm = pe.matmul(ps_kv[:, SLABS * 128:SLABS * 128 + E], turned[:, n.par, n.layer, :],
                               wv_sb[:, n.layer, :], start=False, stop=True, skip_group_check=True)
                mm.then_inc(proj_done, 1)

            def inject_max(n):
                wait(pe, max_done, n, GROUPS, GROUPS)
                for s in range(SLABS):
                    mm = pe.matmul(ps_q[n.par][:, 128 * s:128 * s + 128],
                                   neg_max[:, 8 * s:8 * s + 8, :], ident_bf[:],
                                   start=False, stop=True, skip_group_check=True)
                mm.then_inc(inject_done, 1)

            def attend(n):
                wait(pe, exp_done, n, GROUPS, GROUPS)
                wait(pe, v_done, n, 2, 2)
                for j in range(SLABS * 2):
                    for g in range(GROUPS):
                        head = 8 * (j // 2) + 2 * g + j % 2
                        mm = pe.matmul(attended[32 * g:32 * g + 32, S * j:S * j + S], v_blk[:, n.par, head],
                                       probs[:, n.par, g, j, :], start=(j == 0), stop=True,
                                       skip_group_check=True)
                mm.then_inc(av_done, 1)

            def turn_to_queries(n):
                wait(pe, av_copied, n, 1, 1)
                for s in range(SLABS):
                    mm = pe.transpose(ps_m[:, 256 + 128 * s:256 + 128 * s + 128],
                                      attended_sb[:, 128 * s:128 * s + 128], ident)
                mm.then_inc(av_turned, 1)

            def turn_attended(n):
                wait(pe, attn_done, n, 1, 1)
                for b in range(SPT):
                    for odd in range(2):
                        mm = pe.matmul(attn_turned_ps[S * odd:S * odd + S, S * b:S * b + S],
                                       attn[:, n.par, b].rearrange("p i d -> p (i d)"),
                                       ident[:, S * odd:S * odd + S], start=False, stop=True,
                                       skip_group_check=True)
                mm.then_inc(attn_turned, 1)

            def scores_turned(n, g):
                if g == 0:
                    wait(pe, qblk_done, n, 2, 2)
                rows = slice(32 * g, 32 * g + 32)
                for s in range(SLABS):
                    for b in range(SPT):
                        mm = pe.matmul(ps_s[g][S * b:S * b + S, 2 * S * s:2 * S * s + 2 * S],
                                       k_t[rows, n.par, s, S * b:S * b + S], q_blk[rows, s, b],
                                       start=(s == 0), stop=True, skip_group_check=True)
                mm.then_inc(st_done, 1)

            def turns(n):
                wait(pe, qblk_done, n, 2, -2)
                wait(pe, xn_done, n, 1, 1)
                mm = pe.transpose(ps_q[n.par][:, 256:384], xn[:, n.par, :], ident[:])
                if n.layer:
                    c = Unit(n.number - T, n.pair)
                    if c.pair is None:
                        pe.wait_ge(ld_ctx[c.par], 16 * (c.number // 2 + 1))
                    else:
                        pe.wait_ge(ld_ctx[c.par], c.pair * 16 + 16 * (c.number // 2 + 1))
                    mm = pe.transpose(ps_q[n.par][:, 384:512], ctx_ring[:, n.par, :], ident[:])
                mm.then_inc(turns_done, 1)

            def project_out(n):
                if n.at(2).exists:
                    wait(pe, v_done, n, 2, 6)
                wait(pe, attnt_done, n, 1, 1)
                pe.matmul(y_ps, attn_t[:, n.par, :], wo_sb[:, n.layer, :],
                          start=not n.at(2).exists, stop=True, skip_group_check=True).then_inc(y_done, 1)

            def step(n):
                prev = n.at(-1)
                if n.number <= 0:
                    warm(WARM[n.number + 5])
                if n.exists:
                    scores(n)
                if n.number in (0, 1):
                    warm(8)
                if prev.exists:
                    attend(prev)
                if n.at(1).exists:
                    project_q(n.at(1), 0)
                if n.exists:
                    inject_max(n)
                if n.at(1).exists:
                    project_q(n.at(1), 1)
                if prev.exists:
                    turn_to_queries(prev)
                if n.at(1).exists:
                    project_k(n.at(1))
                if n.exists:
                    pe.matmul(ps_s[0][:], ones_bf[:], zeros[:, 0:256].bitcast(BF16), start=True, stop=True)
                if n.exists:
                    scores_turned(n, 0)
                if n.at(1).exists:
                    project_v(n.at(1))
                if n.exists:
                    scores_turned(n, 1)
                if prev.exists:
                    turn_attended(prev)
                if n.exists:
                    scores_turned(n, 2)
                if n.at(2).exists:
                    turns(n.at(2))
                if n.exists:
                    scores_turned(n, 3)
                if n.exists:
                    wait(pe, exp_done, n, GROUPS, 1)
                    pe.matmul(ps_s[0][:], ones_bf[:], zeros[:, 0:256].bitcast(BF16), start=True, stop=True)
                if prev.exists:
                    project_out(prev)

            run_steps(pe, step)

            pe.wait_ge(exp_done, GROUPS * UNITS)
            for q in range(4):
                for t in range(4 * q, 4 * q + 4):
                    pe.wait_ge(xn3_done, t + 1)
                    mm = pe.transpose(ps_s[q][:, 128 * (t % 4):128 * (t % 4) + 128], xn3[:, t, :], ident[:])
                mm.then_inc(turns3_done, 1)
            pe.wait_ge(qblk_done, 2 * UNITS)
            pe.wait_ge(xt3_done, 4)
            pe.wait_ge(ld_gate, 64)
            for t in range(T):
                mm = pe.matmul(ps_q[0][:, NE * t:NE * t + NE], xt3[:, t, :], wg_sb[:], start=(t == 0), stop=True,
                               skip_group_check=True)
            mm.then_inc(logits_done, 1)
            pe.wait_ge(gate_prep, 2)
            pe.wait_ge(total_done, 1)
            pe.matmul(ps_kv[:, 0:NE], ones_bf[:], first_count_bf[:], start=True, stop=True)
            pe.wait_ge(total_done, 2)
            for k in range(TOP):
                lo = k * T * NE
                pe.matmul(ps_q[1][:, lo:lo + T * NE], tri_bf[:], chosen[:, k].rearrange("p t e -> p (t e)"),
                          start=(k == 0), stop=False, skip_group_check=True)
                for t in range(T - 1):
                    mm = pe.matmul(ps_q[1][:, lo + NE * (t + 1):lo + NE * T], ones_bf[:],
                                   chosen[:, k, t:t + 1, :].to_broadcast([128, T - 1 - t, NE]),
                                   start=False, stop=(t == T - 2), skip_group_check=True)
            mm.then_inc(queue_done, 1)
            pe.wait_ge(facts_done, 4)
            for i in range(KT):
                pe.wait_ge(facts_done, 4 + i + 1)
                mm = pe.matmul(ps_m[:, 0:4 * BLOCKS], at_row[:, i, :], facts[:, i].rearrange("p v i -> p (v i)"),
                               start=(i == 0), stop=(i == KT - 1))
            mm.then_inc(table_done, 1)
            pe.wait_ge(ld_expert, 64)
            pe.wait_ge(rows_done, 2)

            def turn_tokens(e):
                if e >= 2:
                    pe.wait_ge(xet_done, e - 1)
                for i in range(2):
                    pe.wait_ge(gathered[2 * e + i], 16)
                    mm = pe.transpose(ps_x[e % 2][:, 128 * i:128 * i + 128], xe[:, 2 * e + i, :], ident[:])
                mm.then_inc(xe_turned, 1)

            def up(e):
                pe.wait_ge(xet_done, e + 1)
                for c in range(HC):
                    if e >= 2:
                        pe.wait_ge(gelu_done, HC * (e - 2) + 2 * (c // 2) + 2)
                    pe.matmul(ps_s[2 * (e % 2) + c // 2][:, CAP * (c % 2):CAP * (c % 2) + CAP],
                              w1_sb[:, e, 128 * c:128 * c + 128], xe_t[:, e, :], start=(c % 2 == 0), stop=True,
                              skip_group_check=True).then_inc(up_done, 1)

            def down(e):
                if e >= 2:
                    pe.wait_ge(ye_done, e - 1)
                for i in range(2):
                    for c in range(HC):
                        pe.wait_ge(gelu_done, HC * e + c + 1)
                        mm = pe.matmul(ps_y[e % 2][:, E * i:E * i + E], hid[:, e % 2, c, 128 * i:128 * i + 128],
                                       w2_sb[:, e, c, :], start=(i == 0 and c == 0), stop=(c == HC - 1),
                                       skip_group_check=True)
                mm.then_inc(down_done, 1)

            turn_tokens(0)
            for e in range(NE + 1):
                if e + 1 < NE:
                    turn_tokens(e + 1)
                if e < NE:
                    up(e)
                if e >= 1:
                    down(e - 1)


def kernel(**inputs):
    import numpy as np
    import concourse.bacc as bacc
    from concourse.bass_utils import run_bass_kernel_spmd

    def padded(a):
        a = np.asarray(a)
        wide = np.zeros(a.shape[:-1] + (H, SLOT), a.dtype)
        wide[..., 0:D] = a.reshape(a.shape[:-1] + (H, D))
        return wide.reshape(a.shape[:-1] + (H * SLOT,))

    def both(name, turn=False):
        a, b = np.asarray(inputs["L0_attn_" + name]), np.asarray(inputs["L0_xattn_" + name])
        return np.stack([a, b.T if turn else b])

    def columns(a):
        return a.reshape(2, -1, 128).transpose(2, 0, 1).reshape(128, -1)

    def by_parity(a):
        a = a.reshape(2, PAIRS, 2, D, -1).transpose(2, 1, 3, 0, 4)
        return np.ascontiguousarray(a.reshape(128, 2, -1))

    row = np.arange(128)
    arrays = {
        "x_in": np.ascontiguousarray(np.asarray(inputs["x"]).reshape(NSEQ * S, E)),
        "ctx_in": np.ascontiguousarray(np.asarray(inputs["ctx_1024"]).reshape(NSEQ * S, E)),
        "weights": np.ascontiguousarray(np.concatenate(
            [padded(both("Wq", True)), padded(both("Wk", True)), both("Wv", True)], 2).transpose(1, 0, 2)),
        "columns_in": None, "bo": both("bo"),
    }
    arrays["weights"] = np.concatenate([arrays["weights"], by_parity(both("Wo", True))], 2)
    arrays["columns_in"] = np.concatenate([
        np.eye(128), np.stack([row // SLOT % 2 == 0, row // SLOT % 2 == 1, row % SLOT == D], 1),
        columns(padded(both("bq"))), columns(padded(both("bk"))), by_parity(both("bv"))[..., 0]],
        1).astype(np.float32)
    at = np.arange(KT)
    small = np.concatenate([NE - np.arange(NE), np.arange(NE), np.arange(BLOCKS), at % T, at // T])
    arrays["consts_in"] = np.concatenate([
        (row[:, None] <= row[None, :]), np.broadcast_to(row + 1, (128, 128)),
        np.broadcast_to(small, (128, small.size)), row[:, None]], 1).astype(np.float32)
    arrays["wg"] = np.asarray(inputs["L0_ffn_Wg"])
    arrays["w1"] = np.asarray(inputs["L0_ffn_W1"])
    arrays["b1"] = np.ascontiguousarray(np.asarray(inputs["L0_ffn_b1"]).reshape(NE, HC, 128).transpose(2, 0, 1))
    arrays["w2"] = np.asarray(inputs["L0_ffn_W2"])
    arrays["b2"] = np.asarray(inputs["L0_ffn_b2"])
    nc = bacc.Bacc("TRN2", target_bir_lowering=False, num_devices=1)
    args = [nc.dram_tensor(n, a.shape, mybir.dt.from_np(a.dtype), kind="ExternalInput").ap()
            for n, a in arrays.items()]
    out = nc.dram_tensor("out", (NSEQ * S, E), F32, kind="ExternalOutput").ap()
    decoder_layer(nc, *args, out)
    r = run_bass_kernel_spmd(nc, [arrays], core_ids=[0])
    return r.results[0]["out"].reshape(NSEQ, S, E)
```

```python
import concourse.bass as bass
from concourse import mybir
from contextlib import ExitStack

F32 = mybir.dt.float32
BF16 = mybir.dt.bfloat16
U32 = mybir.dt.uint32
ALU = mybir.AluOpType
ACT = mybir.ActivationFunctionType
AX = mybir.AxisListType

NSEQ, S, E = 32, 64, 128
H, D = 16, 8
T = NSEQ * S // 128
SPT = 128 // S
UNITS = 2 * T
PAIRS = H // 2
SLOT = 16
SLABS = H * SLOT // 128
GROUPS = 4
EPS = 1e-5
NE, TOP, HID = 8, 2, 512
CAP = 256
HC = HID // 128
BLOCKS = NE * CAP // 128
KT = TOP * T
ACT_ROWS, ACT_GROUP = 10, 5
POOL_ROWS = 7
QUARTERS = 4
EMPTY = 2 * TOP * NSEQ * S
IDLE_START = 8
IDLE_BEFORE = {-2: 4, -1: 4, 0: 4}
IDLE_AFTER_SCORES = {0: 2, 1: 2}
IDLE_TABLES = 6
IDLE_EXPERTS = 2
SCALE = 1.0 / float(D) ** 0.5


def decoder_layer(nc, x_in, ctx_in, weights, columns_in, bo, consts_in, wg, w1, b1, w2, b2, out):
    ctx = ExitStack()
    with ctx:
        def sb(name, shape, dt=F32):
            return ctx.enter_context(nc.sbuf_tensor(name, shape, dt))

        def bank(name):
            return ctx.enter_context(nc.psum_tensor(name, [128, 512], F32))

        def sem(name):
            return ctx.enter_context(nc.semaphore(name))

        x = sb("x", [128, T // 2, 2, E])
        ctx_ring = sb("ctx_ring", [128, 2, E])
        ident_bf = sb("ident_bf", [128, 128], BF16)
        WIDE = SLABS * 128
        w_sb = sb("w_sb", [128, 2, 2 * WIDE + 2 * E])
        wq_sb, wk_sb = w_sb[:, :, 0:WIDE], w_sb[:, :, WIDE:2 * WIDE]
        wv_sb, wo_sb = w_sb[:, :, 2 * WIDE:2 * WIDE + E], w_sb[:, :, 2 * WIDE + E:]
        columns_sb = sb("columns_sb", [128, 128 + 3 + 4 * SLABS + 2])
        ident = columns_sb[:, 0:128]
        hmask = columns_sb[:, 128:130]
        kone = columns_sb[:, 130:131]
        bq_sb = columns_sb[:, 131:131 + 2 * SLABS].rearrange("p (a s) -> p a s", a=2)
        bk_in = columns_sb[:, 131 + 2 * SLABS:131 + 4 * SLABS].rearrange("p (a s) -> p a s", a=2)
        bv_col = columns_sb[:, 131 + 4 * SLABS:]
        bk_sb = sb("bk_sb", [128, 2, SLABS])
        bq_masked = sb("bq_masked", [128, 2, 2, SLABS, SPT])
        bv_wide = sb("bv_wide", [128, 2, 128])
        bo_rows = sb("bo_rows", [128, 2, E])
        stats = sb("stats", [128, 6])
        meanvar = sb("meanvar", [128, 2, 2])
        logvar = sb("logvar", [128, 2, 1])
        eps_col = sb("eps_col", [128, 1])
        rstd = sb("rstd", [128, 2, 1])
        newton = sb("newton", [128, 2, 5])
        minus_half = sb("minus_half", [128, 1])
        three = sb("three", [128, 1])
        xn = sb("xn", [128, 2, E])
        turned = sb("turned", [128, 2, 2, 128])
        q_bf = sb("q_bf", [128, 2, SLABS, 128], BF16)
        q_blk = sb("q_blk", [128, SLABS, SPT, 2, S])
        k_t = sb("k_t", [128, 2, SLABS, 128])
        k_blk_bf = sb("k_blk_bf", [128, SLABS, SPT, 2, S], BF16)
        v_blk = sb("v_blk", [128, 2, H, SPT, SLOT])
        neg_max = sb("neg_max", [128, H, SLOT], BF16)
        probs = sb("probs", [128, 2, GROUPS, SLABS * 2, S])
        attended_sb = sb("attended_sb", [128, SLABS * 2 * S])
        inv_den = sb("inv_den", [128, SPT, PAIRS])
        attn = sb("attn", [128, 2, SPT, PAIRS, D])
        attn_t = sb("attn_t", [128, 2, 128])

        tri = sb("tri", [128, 128])
        tri_bf = sb("tri_bf", [128, 128], BF16)
        count_row = sb("count_row", [128, 128])
        count_bf = sb("count_bf", [128, 128], BF16)
        small = sb("small", [128, 2 * NE + BLOCKS + KT + 1])
        rank = small[:, 0:NE]
        expert_no = small[:, NE:2 * NE]
        block_no = small[:, 2 * NE:2 * NE + BLOCKS]
        code_no = small[:, 2 * NE + BLOCKS:2 * NE + BLOCKS + KT]
        part_no = small[:, 2 * NE + BLOCKS + KT:]
        ones_bf = sb("ones_bf", [128, 128], BF16)
        wg_sb = sb("wg_sb", [128, NE])
        w1_sb = sb("w1_sb", [128, NE, HID])
        b1_sb = sb("b1_sb", [128, NE, HC])
        w2_sb = sb("w2_sb", [128, NE, HC, E])
        b2_rows = sb("b2_rows", [128, NE, E])
        zeros = sb("zeros", [128, 1024])
        stats3 = sb("stats3", [128, 6])
        meanvar3 = sb("meanvar3", [128, 2, 2])
        logvar3 = sb("logvar3", [128, 2, 1])
        rstd3 = sb("rstd3", [128, 2, 1])
        newton3 = sb("newton3", [128, 2, 5])
        xn3 = sb("xn3", [128, T // 2, 2, E])
        xt3 = sb("xt3", [128, T, 128])
        gate = sb("gate", [128, T, NE])
        gate_tmp = sb("gate_tmp", [128, T, NE])
        gate_col = sb("gate_col", [128, 4, T])
        best = sb("best", [128, TOP, T])
        chosen = sb("chosen", [128, TOP, T, NE], BF16)
        first_count = sb("first_count", [128, NE])
        first_count_bf = sb("first_count_bf", [128, NE], BF16)
        base = sb("base", [128, TOP, NE])
        order = sb("order", [128, TOP, T, NE])
        order_tmp = sb("order_tmp", [128, TOP, T, NE])
        place = sb("place", [128, KT])
        expert = sb("expert", [128, KT])
        upper = sb("upper", [128, KT])
        row_in = sb("row_in", [128, KT])
        blk = sb("blk", [128, KT])
        dropped = sb("dropped", [128, KT])
        part_bf = sb("part_bf", [128, 3, KT], BF16)
        rest = sb("rest", [128, 2, KT])
        apart = sb("apart", [128, 2, ACT_GROUP, 128])
        in_block = sb("in_block", [128, KT, BLOCKS], BF16)
        at_row = sb("at_row", [128, KT, 128], BF16)
        facts = sb("facts", [128, KT, 2, BLOCKS], BF16)
        weight_facts = sb("weight_facts", [128, KT, 3, BLOCKS], BF16)
        table = sb("table", [128, 2, BLOCKS])
        weight_table = sb("weight_table", [128, 3, BLOCKS])
        slot_w = sb("slot_w", [128, 2, BLOCKS])
        slot_row = sb("slot_row", [128, BLOCKS])
        src_f = sb("src_f", [128, 2, BLOCKS])
        dst_f = sb("dst_f", [128, 2, BLOCKS])
        src_row = sb("src_row", [128, BLOCKS], U32)
        dst_row = sb("dst_row", [128, BLOCKS], U32)
        xe = sb("xe", [128, BLOCKS, E])
        xe_t = sb("xe_t", [128, NE, CAP])
        hid = sb("hid", [128, 2, HC, CAP])
        ye = sb("ye", [128, BLOCKS, E])
        answer = sb("answer", [128, 2, E])
        z = sb("z", [128, TOP, T, E])
        xn_rows = nc.dram_tensor("xn_rows", (NSEQ * S, E), F32).ap()
        z_rows = nc.dram_tensor("z_rows", (TOP * NSEQ * S, E), F32).ap()

        ps_q = [bank("ps_q0"), bank("ps_q1")]
        ps_kv = bank("ps_kv")
        ps_s = [bank("ps_s%d" % g) for g in range(GROUPS)]
        ps_m = bank("ps_m")
        attended = ps_m[:, 0:SLABS * 2 * S]
        attended_t = ps_m[:, 256:512].rearrange(
            "p (i b c) -> p i b c", b=SPT, c=SLOT)
        attn_turned_ps = ps_m[:, 0:128]
        y_ps = ps_kv[:, 384:384 + E]

        COLUMNS_READY = 1 + 2 * 4
        BO_READY = COLUMNS_READY + 2
        POOL_READY = 6 + SPT
        ld_const = sem("ld_const")
        ld_w = [sem("ld_w0"), sem("ld_w1")]
        ld_bo = sem("ld_bo")
        ld_x = [sem("ld_x%d" % i) for i in range(QUARTERS)]
        ld_ctx = [sem("ld_ctx0"), sem("ld_ctx1")]
        st_out = sem("st_out")
        prep_pool = sem("prep_pool")
        prep_dve = sem("prep_dve")
        prep_pe = sem("prep_pe")
        bias_added = sem("bias_added")
        stats_done = sem("stats_done")
        aggr_done = sem("aggr_done")
        logvar_done = sem("logvar_done")
        rstd0_done = sem("rstd0_done")
        newton_done = sem("newton_done")
        xn_done = sem("xn_done")
        turns_done = sem("turns_done")
        turned_copied = sem("turned_copied")
        projq_done = sem("projq_done")
        proj_done = sem("proj_done")
        kt_done = sem("kt_done")
        qbf_done = sem("qbf_done")
        kbf_done = sem("kbf_done")
        v_done = sem("v_done")
        s_done = sem("s_done")
        max_done = sem("max_done")
        inject_done = sem("inject_done")
        qblk_done = sem("qblk_done")
        st_done = sem("st_done")
        exp_done = sem("exp_done")
        av_done = sem("av_done")
        av_copied = sem("av_copied")
        av_turned = sem("av_turned")
        inv_done = sem("inv_done")
        attn_done = sem("attn_done")
        attn_turned = sem("attn_turned")
        attnt_done = sem("attnt_done")
        y_done = sem("y_done")
        resid_done = sem("resid_done")

        ld_gate = sem("ld_gate")
        gate_prep = sem("gate_prep")
        ld_expert = sem("ld_expert")
        constants_filled = sem("constants_filled")
        z_cleared = sem("z_cleared")
        st_xn = sem("st_xn")
        gathered = [sem("gathered%d" % i) for i in range(BLOCKS)]
        st_z = sem("st_z")
        ld_z = [[sem("ld_z%d_%d" % (k, q)) for q in range(QUARTERS)] for k in range(TOP)]
        stats3_done = sem("stats3_done")
        aggr3_done = sem("aggr3_done")
        logvar3_done = sem("logvar3_done")
        rstd3_done = sem("rstd3_done")
        newton3_done = sem("newton3_done")
        xn3_done = sem("xn3_done")
        turns3_done = sem("turns3_done")
        xt3_done = sem("xt3_done")
        logits_done = sem("logits_done")
        shifted_done = sem("shifted_done")
        gate_exp_done = sem("gate_exp_done")
        route = sem("route")
        queue_done = sem("queue_done")
        first_done = sem("first_done")
        second_done = sem("second_done")
        row_in_done = sem("row_in_done")
        in_block_done = sem("in_block_done")
        weight_facts_done = sem("weight_facts_done")
        apart_done = sem("apart_done")
        first_rows_done = sem("first_rows_done")
        act_rows_done = sem("act_rows_done")
        last_rows_done = sem("last_rows_done")
        facts_done = sem("facts_done")
        weights_done = sem("weights_done")
        answer_done = sem("answer_done")
        table_done = sem("table_done")
        rows_done = sem("rows_done")
        xe_turned = sem("xe_turned")
        xet_done = sem("xet_done")
        up_done = sem("up_done")
        gelu_done = sem("gelu_done")
        down_done = sem("down_done")
        ye_done = sem("ye_done")
        out_done = [sem("out_done%d" % q) for q in range(QUARTERS)]

        block = ctx.enter_context(nc.Block())
        ps_x = [ps_kv, ps_m]
        ps_y = ps_q

        TURNS = [range(0, 4), range(4, 8), range(8, 12), range(12, 15), range(15, 16)]

        def combine(eng, engine, q):
            rows = x[:, 2 * q:2 * q + 2].rearrange("p i k e -> p (i k) e")
            for k in range(TOP):
                eng.wait_ge(ld_z[k][q], 16)
                if k:
                    eng.wait_ge(out_done[q], k)
                engine.tensor_tensor(rows, rows, z[:, k, 4 * q:4 * q + 4], ALU.add).then_inc(out_done[q], 1)

        class Unit:

            def __init__(self, number, pair=None):
                self.number, self.pair = number, pair
                self.par = number % 2
                self.layer = number // T

            def at(self, k):
                return Unit(self.number + k, self.pair)

            @property
            def exists(self):
                return 0 <= self.number < UNITS

            def tile_pair(self):
                p = (self.number % T) // 2
                return p if self.pair is None else self.pair + p

            def x(self):
                return x[:, self.tile_pair(), self.par, :]

            def count(self, per, extra=0):
                n = per * self.number + extra
                return n if self.pair is None else self.pair * (2 * per) + n

        def wait(eng, semaphore, unit, per, extra=0):
            if per * unit.number + extra > 0:
                eng.wait_ge(semaphore, unit.count(per, extra))
            else:
                assert unit.pair is None

        FIRST, LAST = -3, UNITS + 2
        LOOP_FROM, LOOP_STEPS = 3, 10

        def run_steps(eng, step):
            n = FIRST
            while n <= LAST:
                if n % T == LOOP_FROM and 0 <= n < UNITS:
                    with eng.Fori(0, LOOP_STEPS // 2) as pair:
                        for k in range(2):
                            step(Unit(n + k, pair))
                    n += LOOP_STEPS
                else:
                    step(Unit(n))
                    n += 1

        @block.sync
        def _(sp):
            x_tiles = x_in.rearrange("(i k p) e -> p i k e", k=2, p=128)
            ctx_tiles = ctx_in.rearrange("(i k p) e -> p i k e", k=2, p=128)
            for q in range(QUARTERS):
                if q == 1:
                    sp.wait_ge(ld_w[0], 16)
                sp.dma_start(x[:, 2 * q:2 * q + 2], x_tiles[:, 2 * q:2 * q + 2]).then_inc(ld_x[q], 16)

            sp.wait_ge(ld_w[1], 16)
            sp.wait_ge(ld_x[QUARTERS - 1], 16)
            sp.dma_start(wg_sb[:], wg).then_inc(ld_gate, 16)
            sp.dma_start(tri[:], consts_in[:, 0:128]).then_inc(ld_gate, 16)
            sp.dma_start(count_row[:], consts_in[:, 128:256]).then_inc(ld_gate, 16)
            sp.dma_start(small[:], consts_in[:, 256:]).then_inc(ld_gate, 16)
            sp.dma_start(b1_sb[:], b1).then_inc(ld_expert, 16)
            sp.dma_start(b2_rows[:], b2.rearrange("(q x) e -> q x e", q=1).to_broadcast([128, NE, E]))\
              .then_inc(ld_expert, 16)
            sp.dma_start(w1_sb[:], w1.rearrange("x d h -> d x h")).then_inc(ld_expert, 16)
            sp.dma_start(w2_sb[:], w2.rearrange("x (c p) e -> p x c e", p=128)).then_inc(ld_expert, 16)
            sp.wait_ge(constants_filled, 1)
            z_flat = z_rows.rearrange("(c p r) e -> c p (r e)", p=128, r=8)
            for c in range(TOP * NSEQ * S // 1024):
                sp.dma_start(z_flat[c], zeros[:]).then_inc(z_cleared, 16)

            def load_ctx(u):
                wait(sp, turns_done, u, 1, -1)
                sp.dma_start(ctx_ring[:, u.par, :], ctx_tiles[:, u.tile_pair(), u.par, :])\
                  .then_inc(ld_ctx[u.par], 16)

            for t in range(2):
                load_ctx(Unit(T + t))
            with sp.Fori(0, T // 2 - 1) as pair:
                for k in range(2):
                    load_ctx(Unit(T + 2 + k, pair))
            xn_tiles = xn_rows.rearrange("(i k p) e -> p i k e", k=2, p=128)
            for q in range(QUARTERS):
                sp.wait_ge(xn3_done, 4 * q + 4)
                sp.dma_start(xn_tiles[:, 2 * q:2 * q + 2], xn3[:, 2 * q:2 * q + 2]).then_inc(st_xn, 16)
            z_tiles = z_rows.rearrange("(k t p) e -> p k t e", k=TOP, p=128)
            sp.wait_ge(st_z, 16 * BLOCKS)
            for q in range(QUARTERS):
                tiles = slice(4 * q, 4 * q + 4)
                for k in range(TOP):
                    sp.dma_start(z[:, k, tiles], z_tiles[:, k, tiles]).then_inc(ld_z[k][q], 16)
            out_tiles = out.rearrange("(i k p) e -> p i k e", k=2, p=128)
            for q in range(QUARTERS):
                sp.wait_ge(out_done[q], TOP)
                sp.dma_start(out_tiles[:, 2 * q:2 * q + 2], x[:, 2 * q:2 * q + 2]).then_inc(st_out, 16)
            sp.wait_ge(st_out, 16 * QUARTERS)

        @block.gpsimd
        def _(pool):
            nc.gpsimd.memset(zeros[:], 0.0).then_inc(constants_filled, 1)
            nc.gpsimd.memset(ones_bf[:], 1.0).then_inc(constants_filled, 1)
            nc.gpsimd.memset(v_blk[:], 0.0).then_inc(prep_pool, 1)
            nc.gpsimd.memset(neg_max[:], 0.0).then_inc(prep_pool, 1)
            nc.gpsimd.memset(eps_col[:], EPS).then_inc(prep_pool, 1)
            nc.gpsimd.memset(minus_half[:], -0.5).then_inc(prep_pool, 1)
            nc.gpsimd.memset(three[:], 3.0).then_inc(prep_pool, 1)
            nc.gpsimd.memset(base[:, 0, :], 0.0).then_inc(prep_pool, 1)
            for b in range(SPT):
                pool.wait_ge(prep_pool, 6 + b)
                nc.gpsimd.memset(v_blk[S * b:S * b + S, :, :, b, D], 1.0).then_inc(prep_pool, 1)
            pool.wait_ge(prep_pool, POOL_READY)

            def refine_rstd(u, first, rstd, meanvar, newton, guessed, newton_done):
                v, yy, vyy, less3, half = (newton[:, u.par, i:i + 1] for i in range(5))
                y = rstd[:, u.par, :]
                wait(pool, guessed, u, 1, 1 - first)
                nc.gpsimd.tensor_tensor(v, meanvar[:, u.par, 1:2], eps_col[:], ALU.add).then_inc(newton_done, 1)
                nc.gpsimd.tensor_tensor(yy, y, y, ALU.mult).then_inc(newton_done, 1)
                nc.gpsimd.tensor_tensor(half, y, minus_half[:], ALU.mult).then_inc(newton_done, 1)
                wait(pool, newton_done, u, 6, 3 - 6 * first)
                nc.gpsimd.tensor_tensor(vyy, yy, v, ALU.mult).then_inc(newton_done, 1)
                wait(pool, newton_done, u, 6, 4 - 6 * first)
                nc.gpsimd.tensor_tensor(less3, vyy, three[:], ALU.subtract).then_inc(newton_done, 1)
                wait(pool, newton_done, u, 6, 5 - 6 * first)
                nc.gpsimd.tensor_tensor(y, less3, half, ALU.mult).then_inc(newton_done, 1)

            def step(n):
                u, old, done = n.at(3), n.at(2), n.at(-2)
                if u.exists:
                    refine_rstd(u, 0, rstd, meanvar, newton, rstd0_done, newton_done)
                if old.exists:
                    if old.number == 0:
                        pool.wait_ge(prep_dve, BO_READY)
                    wait(pool, xn_done, old, 1, 1)
                    nc.gpsimd.tensor_tensor(old.x(), old.x(), bo_rows[:, old.layer, :], ALU.add)\
                      .then_inc(bias_added, 1)
                if done.exists and done.layer:
                    refine_rstd(done, T, rstd3, meanvar3, newton3, rstd3_done, newton3_done)

            run_steps(pool, step)

            pool.wait_ge(row_in_done, 1)
            for i in range(KT - POOL_ROWS, KT):
                nc.gpsimd.tensor_scalar(at_row[:, i, :], count_bf[:], row_in[:, i:i + 1], None, ALU.is_equal)\
                    .then_inc(last_rows_done, 1)
            pool.wait_ge(rows_done, 2)
            pool.wait_ge(st_xn, 16 * QUARTERS)
            for i in range(BLOCKS):
                pool.indirect_dma_start(out=xe[:, i, :], out_offset=None, in_=xn_rows,
                                        in_offset=bass.IndirectOffsetOnAxis(ap=src_row[:, i:i + 1], axis=0))\
                    .then_inc(gathered[i], 16)
            pool.wait_ge(z_cleared, 16 * (TOP * NSEQ * S // 1024))
            for i in range(BLOCKS):
                pool.wait_ge(ye_done, i + 1)
                pool.indirect_dma_start(out=z_rows,
                                        out_offset=bass.IndirectOffsetOnAxis(ap=dst_row[:, i:i + 1], axis=0),
                                        in_=ye[:, i, :], in_offset=None,
                                        bounds_check=TOP * NSEQ * S - 1, oob_is_err=False)\
                    .then_inc(st_z, 16)
            combine(pool, nc.gpsimd, 0)

        @block.vector
        def _(dve):
            dve.wait_ge(ld_const, 16)
            nc.vector.tensor_copy(ident_bf[:], ident[:]).then_inc(prep_dve, 1)
            for a in range(2):
                nc.vector.tensor_scalar(bk_sb[:, a, :], bk_in[:, a, :], kone[:, 0:1], None, ALU.add)\
                  .then_inc(prep_dve, 1)
                nc.vector.tensor_copy(bv_wide[:, a, :], bv_col[:, a:a + 1].to_broadcast([128, 128]))\
                  .then_inc(prep_dve, 1)
                for hh in range(2):
                    nc.vector.tensor_scalar(bq_masked[:, a, hh],
                                            bq_sb[:, a, :].unsqueeze(2).to_broadcast([128, SLABS, SPT]),
                                            hmask[:, hh:hh + 1], None, ALU.mult).then_inc(prep_dve, 1)
            def step(n):
                ln, nx2, nxt, prev, old, done = (n.at(k) for k in (3, 2, 1, -1, -2, -3))
                if n.number == UNITS:
                    dve.wait_ge(ld_gate, 64)
                    nc.vector.tensor_copy(tri_bf[:], tri[:]).then_inc(gate_prep, 1)
                    nc.vector.tensor_copy(count_bf[:], count_row[:]).then_inc(gate_prep, 1)
                if ln.exists:
                    if ln.layer == 0:
                        if ln.pair is None:
                            dve.wait_ge(ld_x[ln.number // 4], 16)
                        else:
                            for q in ld_x:
                                dve.wait_ge(q, 16)
                    else:
                        wait(dve, resid_done, ln, 1, -T + 1)
                    wait(dve, aggr_done, ln, 1, 0)
                    nc.vector.bn_stats(stats[:], ln.x()).then_inc(stats_done, 1)
                    wait(dve, stats_done, ln, 1, 1)
                    wait(dve, xn_done, ln, 1, -1)

                def normalise3(done):
                    if done.exists and done.layer:
                        wait(dve, newton3_done, done, 6, 6 - 6 * T)
                        nc.vector.tensor_scalar(xn3[:, done.tile_pair(), done.par, :], done.x(),
                                                meanvar3[:, done.par, 0:1], rstd3[:, done.par, :],
                                                ALU.subtract, ALU.mult).then_inc(xn3_done, 1)

                def group_max(g):
                    wait(dve, s_done, n, GROUPS, g + 1)
                    nc.vector.tensor_reduce(
                        neg_max[:].rearrange("p (s g j) c -> p s g j c", s=SLABS, g=GROUPS)[:, :, g, :, D],
                        ps_s[g][:, 0:SLABS * 2 * S].rearrange("p (s j k) -> p s j k", s=SLABS, k=S),
                        AX.X, ALU.max, negate=True).then_inc(max_done, 1)

                if n.exists:
                    if n.number == 0:
                        dve.wait_ge(prep_pool, POOL_READY)
                    wait(dve, inject_done, n, 1, 0)
                    for g in range(GROUPS):
                        group_max(g)
                if ln.exists:
                    nc.vector.bn_aggr(meanvar[:, ln.par, :], stats[:]).then_inc(aggr_done, 1)
                if old.exists:
                    wait(dve, y_done, old, 1, 1)
                    wait(dve, bias_added, old, 1, 1)
                    nc.vector.tensor_tensor(old.x(), old.x(), y_ps, ALU.add)\
                      .then_inc(resid_done, 1)
                if n.exists:
                    wait(dve, inject_done, n, 1, 1)
                    for hh in range(2):
                        nc.vector.scalar_tensor_tensor(
                            out=q_blk[:, :, :, hh, :],
                            in0=ps_q[n.par][:, 0:SLABS * 128].rearrange("p (s b t) -> p s b t", s=SLABS, b=SPT),
                            scalar=hmask[:, hh:hh + 1],
                            in1=bq_masked[:, n.layer, hh].unsqueeze(3).to_broadcast([128, SLABS, SPT, S]),
                            op0=ALU.mult, op1=ALU.add).then_inc(qblk_done, 1)
                if prev.exists:
                    wait(dve, av_turned, prev, 1, 1)
                    nc.vector.reciprocal(inv_den[:], attended_t[:, :, :, D].rearrange("p i b -> p b i"))\
                      .then_inc(inv_done, 1)
                    wait(dve, inv_done, prev, 1, 1)
                    nc.vector.tensor_tensor(
                        attn[:, prev.par], attended_t[:, :, :, 0:D].rearrange("p i b d -> p b i d"),
                        inv_den[:].unsqueeze(3).to_broadcast([128, SPT, PAIRS, D]),
                        ALU.mult).then_inc(attn_done, 1)
                if nx2.exists:
                    wait(dve, newton_done, nx2, 6, 6)
                    wait(dve, turns_done, nx2, 1, -1)
                    nc.vector.tensor_scalar(xn[:, nx2.par, :], nx2.x(), meanvar[:, nx2.par, 0:1],
                                            rstd[:, nx2.par, :], ALU.subtract, ALU.mult).then_inc(xn_done, 1)
                if old.exists and old.layer:
                    wait(dve, resid_done, old, 1, 1)
                    wait(dve, aggr3_done, old, 1, -T)
                if n.exists:
                    normalise3(done)
                if old.exists and old.layer:
                    nc.vector.bn_stats(stats3[:], old.x()).then_inc(stats3_done, 1)
                if nxt.exists:
                    wait(dve, projq_done, nxt, SLABS, SLABS)
                    nc.vector.tensor_tensor(
                        q_bf[:, nxt.par], ps_q[nxt.par][:, 0:SLABS * 128].rearrange("p (s t) -> p s t", s=SLABS),
                        bq_sb[:, nxt.layer, :].unsqueeze(2).to_broadcast([128, SLABS, 128]),
                        ALU.add).then_inc(qbf_done, 1)
                    wait(dve, kt_done, nxt, SLABS, SLABS)
                    wait(dve, s_done, n, GROUPS, GROUPS)
                if old.exists and old.layer:
                    wait(dve, stats3_done, old, 1, 1 - T)
                if nxt.exists:
                    for hh in range(2):
                        nc.vector.tensor_scalar(
                            k_blk_bf[:, :, :, hh, :],
                            k_t[:, nxt.par].rearrange("p s (b t) -> p s b t", b=SPT),
                            hmask[:, hh:hh + 1], None, ALU.mult).then_inc(kbf_done, 1)
                if old.exists and old.layer:
                    nc.vector.bn_aggr(meanvar3[:, old.par, :], stats3[:]).then_inc(aggr3_done, 1)
                if not n.exists:
                    normalise3(done)
                if n.number == -1:
                    dve.wait_ge(prep_pe, 1)
                    dve.wait_ge(ld_bo, 16)
                    for a in range(2):
                        nc.vector.tensor_tensor(bo_rows[:, a, :], bo_rows[:, a, :],
                                                ps_s[1][:, a * E:a * E + E], ALU.add).then_inc(prep_dve, 1)

            run_steps(dve, step)

            steps = [0]

            def then(*instructions):
                for ins in instructions:
                    steps[0] += 1
                    ins.then_inc(route, 1)
                dve.wait_ge(route, steps[0])

            def wide(col):
                return col.unsqueeze(2).to_broadcast([128, T, NE])

            dve.wait_ge(logits_done, T)
            logits = ps_q[0][:, 0:T * NE].rearrange("p (t e) -> p t e", e=NE)
            then(nc.vector.tensor_reduce(gate_col[:, 0], logits, AX.X, ALU.max))
            nc.vector.tensor_tensor(gate[:], logits, wide(gate_col[:, 0]), ALU.subtract)\
                .then_inc(shifted_done, 1)
            dve.wait_ge(gate_exp_done, 1)
            then(nc.vector.tensor_reduce(gate_col[:, 1], gate[:], AX.X, ALU.add))
            then(nc.vector.reciprocal(gate_col[:, 2], gate_col[:, 1]))
            then(nc.vector.tensor_tensor(gate[:], gate[:], wide(gate_col[:, 2]), ALU.mult))
            for k in range(TOP):
                then(nc.vector.tensor_reduce(best[:, k, :], gate[:], AX.X, ALU.max))
                then(nc.vector.tensor_tensor(gate_tmp[:], gate[:], wide(best[:, k, :]), ALU.is_equal))
                then(nc.vector.tensor_tensor(gate_tmp[:], gate_tmp[:],
                                             rank.unsqueeze(1).to_broadcast([128, T, NE]), ALU.mult))
                then(nc.vector.tensor_reduce(gate_col[:, 3], gate_tmp[:], AX.X, ALU.max))
                then(nc.vector.tensor_tensor(chosen[:, k], gate_tmp[:], wide(gate_col[:, 3]), ALU.is_equal))
                if k == 0:
                    then(nc.vector.scalar_tensor_tensor(out=gate[:], in0=chosen[:, 0], scalar=-2.0, in1=gate[:],
                                                        op0=ALU.mult, op1=ALU.add),
                         nc.vector.tensor_reduce(first_count[:], chosen[:, 0].rearrange("p t e -> p e t"),
                                                 AX.X, ALU.add))
                    nc.vector.tensor_copy(first_count_bf[:], first_count[:]).then_inc(first_done, 1)
            pair_weights = best[:].rearrange("p k t -> p (k t)")
            picks, picks_tmp, queues = (a[:].rearrange("p k t e -> p (k t) e") for a in (chosen, order_tmp, order))
            wsum, wsum_eps, winv = gate_col[:, 0], gate_col[:, 1], gate_col[:, 2]
            nc.vector.tensor_tensor(wsum, best[:, 0, :], best[:, 1, :], ALU.add).then_inc(second_done, 1)
            dve.wait_ge(second_done, 1)
            then(nc.vector.tensor_tensor(picks_tmp, picks, expert_no.unsqueeze(1).to_broadcast([128, KT, NE]),
                                         ALU.mult),
                 nc.vector.tensor_scalar(wsum_eps, wsum, 1e-9, None, ALU.add))
            then(nc.vector.tensor_reduce(expert[:], picks_tmp, AX.X, ALU.add),
                 nc.vector.reciprocal(winv, wsum_eps))
            dve.wait_ge(queue_done, 1)
            then(nc.vector.tensor_scalar(base[:, 1, :], ps_kv[:, 0:NE], float(CAP), None, ALU.min),
                 nc.vector.tensor_tensor(best[:], best[:], winv.unsqueeze(1).to_broadcast([128, TOP, T]),
                                         ALU.mult))
            then(nc.vector.tensor_tensor(order[:], ps_q[1][:, 0:KT * NE].rearrange("p (k t e) -> p k t e", t=T, e=NE),
                                         base[:].unsqueeze(2).to_broadcast([128, TOP, T, NE]), ALU.add),
                 nc.vector.tensor_copy(part_bf[:, 0], pair_weights))
            then(nc.vector.tensor_tensor(order[:], order[:], chosen[:], ALU.mult),
                 nc.vector.tensor_tensor(rest[:, 0], pair_weights, part_bf[:, 0], ALU.subtract))
            then(nc.vector.tensor_reduce(place[:], queues, AX.X, ALU.add),
                 nc.vector.tensor_copy(part_bf[:, 1], rest[:, 0]))
            then(nc.vector.tensor_scalar(upper[:], place[:], 128.5, None, ALU.is_gt),
                 nc.vector.tensor_scalar(dropped[:], place[:], CAP + 0.5, None, ALU.is_gt),
                 nc.vector.tensor_tensor(rest[:, 1], rest[:, 0], part_bf[:, 1], ALU.subtract))
            nc.vector.scalar_tensor_tensor(out=row_in[:], in0=upper[:], scalar=-128.0, in1=place[:],
                                           op0=ALU.mult, op1=ALU.add).then_inc(row_in_done, 1)
            then(nc.vector.scalar_tensor_tensor(out=blk[:], in0=expert[:], scalar=float(CAP // 128), in1=upper[:],
                                                op0=ALU.mult, op1=ALU.add),
                 nc.vector.tensor_copy(part_bf[:, 2], rest[:, 1]))
            then(nc.vector.scalar_tensor_tensor(out=blk[:], in0=dropped[:], scalar=float(4 * BLOCKS), in1=blk[:],
                                                op0=ALU.mult, op1=ALU.add))
            nc.vector.tensor_tensor(in_block[:], block_no.unsqueeze(1).to_broadcast([128, KT, BLOCKS]),
                                    blk[:].unsqueeze(2).to_broadcast([128, KT, BLOCKS]), ALU.is_equal)\
                .then_inc(in_block_done, 1)
            dve.wait_ge(in_block_done, 1)
            nc.vector.tensor_scalar(facts[:, :, 0, :], in_block[:], part_no, None, ALU.mult)\
                .then_inc(facts_done, 1)
            nc.vector.tensor_tensor(facts[:, :, 1, :], in_block[:],
                                    code_no.unsqueeze(2).to_broadcast([128, KT, BLOCKS]), ALU.mult)\
                .then_inc(facts_done, 1)
            dve.wait_ge(row_in_done, 1)
            for i in range(KT - POOL_ROWS - ACT_ROWS):
                nc.vector.tensor_scalar(at_row[:, i, :], count_bf[:], row_in[:, i:i + 1], None, ALU.is_equal)\
                    .then_inc(first_rows_done, 1)
            dve.wait_ge(table_done, 1)
            then(nc.vector.tensor_copy(table[:], ps_m[:, 0:2 * BLOCKS].rearrange("p (v i) -> p v i", v=2)))
            then(nc.vector.scalar_tensor_tensor(out=slot_row[:], in0=table[:, 1], scalar=128.0, in1=table[:, 0],
                                                op0=ALU.mult, op1=ALU.add))
            then(nc.vector.tensor_scalar(src_f[:, 0], slot_row[:], NSEQ * S + 127.5, -float(NSEQ * S),
                                         ALU.is_gt, ALU.mult),
                 nc.vector.tensor_scalar(dst_f[:, 0], slot_row[:], 127.5, float(EMPTY), ALU.is_lt, ALU.mult))
            then(nc.vector.scalar_tensor_tensor(out=src_f[:, 1], in0=slot_row[:], scalar=-128.0, in1=src_f[:, 0],
                                                op0=ALU.add, op1=ALU.add))
            nc.vector.tensor_scalar(src_row[:], src_f[:, 1], 0.0, None, ALU.max).then_inc(rows_done, 1)
            nc.vector.scalar_tensor_tensor(out=dst_row[:], in0=slot_row[:], scalar=-128.0, in1=dst_f[:, 0],
                                           op0=ALU.add, op1=ALU.add).then_inc(rows_done, 1)
            for j in range(3):
                nc.vector.tensor_tensor(weight_facts[:, :, j, :], in_block[:],
                                        part_bf[:, j, :].unsqueeze(2).to_broadcast([128, KT, BLOCKS]), ALU.mult)\
                    .then_inc(weight_facts_done, 1)
            dve.wait_ge(table_done, 2)
            then(nc.vector.tensor_copy(weight_table[:],
                                       ps_q[1][:, 0:3 * BLOCKS].rearrange("p (v i) -> p v i", v=3)))
            then(nc.vector.tensor_tensor(slot_w[:, 0], weight_table[:, 0], weight_table[:, 1], ALU.add))
            nc.vector.tensor_tensor(slot_w[:, 1], slot_w[:, 0], weight_table[:, 2], ALU.add)\
                .then_inc(weights_done, 1)

            def expert_tokens(e):
                dve.wait_ge(xe_turned, e + 1)
                nc.vector.tensor_copy(xe_t[:, e, :], ps_x[e % 2][:, 0:CAP]).then_inc(xet_done, 1)

            def expert_answer(e):
                for i in range(2):
                    dve.wait_ge(down_done, 2 * e + i + 1)
                    nc.vector.tensor_tensor(answer[:, i, :], ps_y[i][:, 0:E], b2_rows[:, e, :], ALU.add)\
                        .then_inc(answer_done, 1)
                    dve.wait_ge(answer_done, 2 * e + i + 1)
                    nc.vector.tensor_scalar(ye[:, 2 * e + i, :], answer[:, i, :],
                                            slot_w[:, 1, 2 * e + i:2 * e + i + 1], None, ALU.mult)\
                        .then_inc(ye_done, 1)

            dve.wait_ge(ld_expert, 64)
            dve.wait_ge(weights_done, 1)
            for e in range(NE + 2):
                if e < NE:
                    expert_tokens(e)
                if e >= 2:
                    expert_answer(e - 2)
            for q in range(1, QUARTERS):
                combine(dve, nc.vector, q)

        @block.scalar
        def _(act):
            act.dma_start(columns_sb[:], columns_in).then_inc(ld_const, 16)
            for a in range(2):
                act.dma_start(w_sb[:, a], weights[:, a]).then_inc(ld_w[a], 16)
            act.dma_start(bo_rows[:], bo.rearrange("(q a) n -> q a n", q=1).to_broadcast([128, 2, E]))\
               .then_inc(ld_bo, 16)

            act.preload_act_table_set("natural_log_exp_and_others")
            act.wait_ge(prep_pool, POOL_READY)
            act.wait_ge(prep_dve, COLUMNS_READY)

            def copy_turned(i):
                tiles = TURNS[i]
                act.wait_ge(turns3_done, i + 1)
                act.activation(xt3[:, tiles[0]:tiles[-1] + 1, :],
                               ps_s[i % GROUPS][:, 0:128 * len(tiles)].rearrange("p (t n) -> p t n", n=128),
                               ACT.Copy).then_inc(xt3_done, 1)

            def step(n):
                nxt, prev, ln, done = n.at(1), n.at(-1), n.at(3), n.at(-2)
                if nxt.exists:
                    wait(act, turns_done, nxt, 1, 1)
                    wait(act, proj_done, nxt, 1, -1)
                    act.activation(turned[:, nxt.par, 0:1 + nxt.layer, :],
                                   ps_q[nxt.par][:, 256:256 + 128 * (1 + nxt.layer)].rearrange(
                                       "p (j t) -> p j t", t=128), ACT.Copy).then_inc(turned_copied, 1)
                if prev.exists:
                    wait(act, av_done, prev, 1, 1)
                    act.activation(attended_sb[:], attended, ACT.Copy).then_inc(av_copied, 1)
                if n.number == UNITS:
                    copy_turned(0)

                def exponentials(g):
                    wait(act, st_done, n, GROUPS, g + 1)
                    act.activation(probs[:, n.par, g], ps_s[g][:, 0:SLABS * 2 * S].rearrange(
                        "p (j q) -> p j q", q=S), ACT.Exp, scale=SCALE).then_inc(exp_done, 1)

                if n.exists:
                    exponentials(0)
                if nxt.exists:
                    wait(act, proj_done, nxt, 1, 1)
                    wait(act, st_done, nxt, GROUPS, -GROUPS)
                    for s in range(SLABS):
                        act.activation(k_t[:, nxt.par, s, :], ps_kv[:, 128 * s:128 * s + 128],
                                       ACT.Identity, bias=bk_sb[:, nxt.layer, s:s + 1]).then_inc(kt_done, 1)
                if ln.exists:
                    wait(act, aggr_done, ln, 1, 1)
                    act.activation(logvar[:, ln.par, :], meanvar[:, ln.par, 1:2], ACT.Ln,
                                   bias=eps_col[:, 0:1]).then_inc(logvar_done, 1)
                if n.exists:
                    exponentials(1)
                if ln.exists:
                    wait(act, logvar_done, ln, 1, 1)
                    act.activation(rstd[:, ln.par, :], logvar[:, ln.par, :], ACT.Exp, scale=-0.5)\
                       .then_inc(rstd0_done, 1)
                if prev.exists:
                    wait(act, attn_turned, prev, 1, 1)
                    act.activation(attn_t[:, prev.par, :], attn_turned_ps, ACT.Copy).then_inc(attnt_done, 1)
                if n.number == UNITS:
                    copy_turned(1)
                    copy_turned(2)
                if nxt.exists:
                    wait(act, av_done, n, 1, 0)
                    for b in range(SPT):
                        rows = slice(S * b, S * b + S)
                        act.activation(v_blk[rows, nxt.par, :, b, 0:D],
                                       ps_kv[rows, SLABS * 128:SLABS * 128 + 128].rearrange(
                                           "p (h d) -> p h d", d=D), ACT.Copy).then_inc(v_done, 1)
                if n.exists:
                    exponentials(2)
                if done.exists and done.layer:
                    wait(act, aggr3_done, done, 1, 1 - T)
                    act.activation(logvar3[:, done.par, :], meanvar3[:, done.par, 1:2], ACT.Ln,
                                   bias=eps_col[:, 0:1]).then_inc(logvar3_done, 1)
                if n.exists:
                    exponentials(3)
                if done.exists and done.layer:
                    wait(act, logvar3_done, done, 1, 1 - T)
                    act.activation(rstd3[:, done.par, :], logvar3[:, done.par, :], ACT.Exp, scale=-0.5)\
                       .then_inc(rstd3_done, 1)

            run_steps(act, step)

            copy_turned(3)
            copy_turned(4)
            act.wait_ge(shifted_done, 1)
            act.activation(gate[:], gate[:], ACT.Exp).then_inc(gate_exp_done, 1)
            act.preload_act_table(ACT.Gelu_apprx_tanh)
            act.wait_ge(row_in_done, 1)
            for g in range(ACT_ROWS // ACT_GROUP):
                at = KT - POOL_ROWS - ACT_ROWS + ACT_GROUP * g
                for i in range(ACT_GROUP):
                    act.activation(apart[:, g % 2, i, :], count_bf[:], ACT.Abs, scale=-1.0,
                                   bias=row_in[:, at + i:at + i + 1]).then_inc(apart_done, 1)
                act.wait_ge(apart_done, ACT_GROUP * (g + 1))
                act.activation(at_row[:, at:at + ACT_GROUP, :], apart[:, g % 2], ACT.Relu, scale=-1.0, bias=1.0)\
                   .then_inc(act_rows_done, 1)
            act.wait_ge(ld_expert, 64)
            for e in range(NE):
                for c in range(HC):
                    act.wait_ge(up_done, HC * e + 2 * (c // 2) + 2)
                    if e >= 2 and c == 0:
                        act.wait_ge(down_done, 2 * (e - 1))
                    act.activation(hid[:, e % 2, c, :],
                                   ps_s[2 * (e % 2) + c // 2][:, CAP * (c % 2):CAP * (c % 2) + CAP],
                                   ACT.Gelu_apprx_tanh, bias=b1_sb[:, e, c:c + 1]).then_inc(gelu_done, 1)

        @block.tensor
        def _(pe):
            def idle(count, into):
                for _ in range(count):
                    pe.matmul(into[:], ones_bf[:], zeros[:, 0:256].bitcast(BF16), start=True, stop=True)

            pe.wait_ge(constants_filled, 2)
            idle(IDLE_START, ps_m)
            pe.wait_ge(ld_const, 16)

            def scores(n):
                wait(pe, qbf_done, n, 1, 1)
                wait(pe, kbf_done, n, 2, 2)
                for g in range(GROUPS):
                    wait(pe, exp_done, n, GROUPS, -GROUPS + g + 1)
                    rows = slice(32 * g, 32 * g + 32)
                    for s in range(SLABS):
                        for b in range(SPT):
                            mm = pe.matmul(ps_s[g][S * b:S * b + S, 2 * S * s:2 * S * s + 2 * S],
                                           q_bf[rows, n.par, s, S * b:S * b + S], k_blk_bf[rows, s, b],
                                           start=(s == 0), stop=True, skip_group_check=True)
                    mm.then_inc(s_done, 1)

            def project_q(n, s):
                if s == 0:
                    if n.number == 0:
                        pe.wait_ge(ld_w[0], 16)
                    wait(pe, turned_copied, n, 1, 1)
                pe.matmul(ps_q[n.par][:, 128 * s:128 * s + 128],
                          wq_sb[:, n.layer, 128 * s:128 * s + 128], turned[:, n.par, 0, :],
                          start=(s == 0), stop=False, skip_group_check=True).then_inc(projq_done, 1)

            def project_k(n):
                wait(pe, resid_done, n, 1, -2)
                wait(pe, kt_done, n, SLABS, 0)
                wait(pe, v_done, n, 2, 0)
                for s in range(SLABS):
                    pe.matmul(ps_kv[:, 128 * s:128 * s + 128],
                              wk_sb[:, n.layer, 128 * s:128 * s + 128], turned[:, n.par, n.layer, :],
                              start=(s == 0), stop=True, skip_group_check=True)

            def project_v(n):
                mm = pe.matmul(ps_kv[:, SLABS * 128:SLABS * 128 + E], turned[:, n.par, n.layer, :],
                               wv_sb[:, n.layer, :], start=False, stop=True, skip_group_check=True)
                mm.then_inc(proj_done, 1)

            def inject_max(n):
                wait(pe, max_done, n, GROUPS, GROUPS)
                for s in range(SLABS):
                    mm = pe.matmul(ps_q[n.par][:, 128 * s:128 * s + 128],
                                   neg_max[:, 8 * s:8 * s + 8, :], ident_bf[:],
                                   start=False, stop=True, skip_group_check=True)
                mm.then_inc(inject_done, 1)

            def attend(n):
                wait(pe, exp_done, n, GROUPS, GROUPS)
                wait(pe, v_done, n, 2, 2)
                for j in range(SLABS * 2):
                    for g in range(GROUPS):
                        head = 8 * (j // 2) + 2 * g + j % 2
                        mm = pe.matmul(attended[32 * g:32 * g + 32, S * j:S * j + S], v_blk[:, n.par, head],
                                       probs[:, n.par, g, j, :], start=(j == 0), stop=True,
                                       skip_group_check=True)
                mm.then_inc(av_done, 1)

            def turn_to_queries(n):
                wait(pe, av_copied, n, 1, 1)
                for s in range(SLABS):
                    mm = pe.transpose(ps_m[:, 256 + 128 * s:256 + 128 * s + 128],
                                      attended_sb[:, 128 * s:128 * s + 128], ident)
                mm.then_inc(av_turned, 1)

            def turn_attended(n):
                wait(pe, attn_done, n, 1, 1)
                for b in range(SPT):
                    for odd in range(2):
                        mm = pe.matmul(attn_turned_ps[S * odd:S * odd + S, S * b:S * b + S],
                                       attn[:, n.par, b].rearrange("p i d -> p (i d)"),
                                       ident[:, S * odd:S * odd + S], start=False, stop=True,
                                       skip_group_check=True)
                mm.then_inc(attn_turned, 1)

            def scores_turned(n, g):
                if g == 0:
                    wait(pe, qblk_done, n, 2, 2)
                rows = slice(32 * g, 32 * g + 32)
                for s in range(SLABS):
                    for b in range(SPT):
                        mm = pe.matmul(ps_s[g][S * b:S * b + S, 2 * S * s:2 * S * s + 2 * S],
                                       k_t[rows, n.par, s, S * b:S * b + S], q_blk[rows, s, b],
                                       start=(s == 0), stop=True, skip_group_check=True)
                mm.then_inc(st_done, 1)

            def turns(n):
                wait(pe, qblk_done, n, 2, -2)
                wait(pe, xn_done, n, 1, 1)
                mm = pe.transpose(ps_q[n.par][:, 256:384], xn[:, n.par, :], ident[:])
                if n.layer:
                    c = Unit(n.number - T, n.pair)
                    if c.pair is None:
                        pe.wait_ge(ld_ctx[c.par], 16 * (c.number // 2 + 1))
                    else:
                        pe.wait_ge(ld_ctx[c.par], c.pair * 16 + 16 * (c.number // 2 + 1))
                    mm = pe.transpose(ps_q[n.par][:, 384:512], ctx_ring[:, n.par, :], ident[:])
                mm.then_inc(turns_done, 1)

            def project_out(n):
                if n.at(2).exists:
                    wait(pe, v_done, n, 2, 6)
                wait(pe, attnt_done, n, 1, 1)
                pe.matmul(y_ps, attn_t[:, n.par, :], wo_sb[:, n.layer, :],
                          start=not n.at(2).exists, stop=True, skip_group_check=True).then_inc(y_done, 1)

            def turn_normalised(i):
                pe.wait_ge(exp_done, GROUPS * UNITS)
                if i >= GROUPS:
                    pe.wait_ge(xt3_done, i - GROUPS + 1)
                for j, t in enumerate(TURNS[i]):
                    pe.wait_ge(xn3_done, t + 1)
                    mm = pe.transpose(ps_s[i % GROUPS][:, 128 * j:128 * j + 128], xn3[:, t // 2, t % 2, :], ident)
                mm.then_inc(turns3_done, 1)

            def gate_logits(i):
                if i == 0:
                    pe.wait_ge(qblk_done, 2 * UNITS)
                    pe.wait_ge(ld_gate, 64)
                pe.wait_ge(xt3_done, i + 1)
                for t in TURNS[i]:
                    pe.matmul(ps_q[0][:, NE * t:NE * t + NE], xt3[:, t, :], wg_sb[:], start=(t == 0), stop=True,
                              skip_group_check=True).then_inc(logits_done, 1)

            def step(n):
                prev = n.at(-1)
                idle(IDLE_BEFORE.get(n.number, 0), ps_m)
                if n.number == 0:
                    pe.wait_ge(prep_dve, BO_READY)
                if n.exists:
                    scores(n)
                idle(IDLE_AFTER_SCORES.get(n.number, 0), ps_m)
                if prev.exists:
                    attend(prev)
                if n.number == UNITS:
                    turn_normalised(0)
                if n.at(1).exists:
                    project_q(n.at(1), 0)
                if n.exists:
                    inject_max(n)
                if n.at(1).exists:
                    project_q(n.at(1), 1)
                if prev.exists:
                    turn_to_queries(prev)
                if n.number == UNITS:
                    turn_normalised(1)
                    turn_normalised(2)
                if n.at(1).exists:
                    project_k(n.at(1))
                if n.exists:
                    idle(1, ps_s[0])
                    scores_turned(n, 0)
                if n.at(1).exists:
                    project_v(n.at(1))
                if n.exists:
                    scores_turned(n, 1)
                if prev.exists:
                    turn_attended(prev)
                if n.number == UNITS:
                    gate_logits(0)
                if n.exists:
                    scores_turned(n, 2)
                if n.at(2).exists:
                    turns(n.at(2))
                if n.number == -1:
                    for a in range(2):
                        pe.wait_ge(prep_dve, COLUMNS_READY)
                        pe.wait_ge(ld_w[a], 16)
                        mm = pe.matmul(ps_s[1][:, a * E:a * E + E], bv_wide[:, a, :], wo_sb[:, a, :],
                                       start=(a == 0), stop=True, skip_group_check=True)
                    mm.then_inc(prep_pe, 1)
                if n.exists:
                    scores_turned(n, 3)
                    wait(pe, exp_done, n, GROUPS, 1)
                    idle(1, ps_s[0])
                if prev.exists:
                    project_out(prev)
                if n.number == UNITS:
                    gate_logits(1)
                    gate_logits(2)

            run_steps(pe, step)

            turn_normalised(3)
            gate_logits(3)
            turn_normalised(4)
            gate_logits(4)
            pe.wait_ge(gate_prep, 2)
            pe.wait_ge(first_done, 1)
            pe.matmul(ps_kv[:, 0:NE], ones_bf[:], first_count_bf[:], start=True, stop=True)
            for k in range(TOP):
                if k:
                    pe.wait_ge(second_done, 1)
                lo = k * T * NE
                pe.matmul(ps_q[1][:, lo:lo + T * NE], tri_bf[:], chosen[:, k].rearrange("p t e -> p (t e)"),
                          start=(k == 0), stop=False, skip_group_check=True)
                for t in range(T - 1):
                    mm = pe.matmul(ps_q[1][:, lo + NE * (t + 1):lo + NE * T], ones_bf[:],
                                   chosen[:, k, t:t + 1, :].to_broadcast([128, T - 1 - t, NE]),
                                   start=False, stop=(t == T - 2), skip_group_check=True)
            mm.then_inc(queue_done, 1)
            pe.wait_ge(facts_done, 2)
            for i in range(KT):
                if i < KT - POOL_ROWS - ACT_ROWS:
                    pe.wait_ge(first_rows_done, i + 1)
                elif i < KT - POOL_ROWS:
                    pe.wait_ge(act_rows_done, (i - (KT - POOL_ROWS - ACT_ROWS)) // ACT_GROUP + 1)
                else:
                    pe.wait_ge(last_rows_done, i - (KT - POOL_ROWS) + 1)
                mm = pe.matmul(ps_m[:, 0:2 * BLOCKS], at_row[:, i, :], facts[:, i].rearrange("p v i -> p (v i)"),
                               start=(i == 0), stop=(i == KT - 1))
            mm.then_inc(table_done, 1)
            pe.wait_ge(xt3_done, len(TURNS))
            idle(IDLE_TABLES, ps_s[0])
            pe.wait_ge(weight_facts_done, 3)
            for i in range(KT):
                mm = pe.matmul(ps_q[1][:, 0:3 * BLOCKS], at_row[:, i, :],
                               weight_facts[:, i].rearrange("p v i -> p (v i)"),
                               start=(i == 0), stop=(i == KT - 1))
            mm.then_inc(table_done, 1)
            idle(IDLE_EXPERTS, ps_s[0])
            pe.wait_ge(ld_expert, 64)
            pe.wait_ge(rows_done, 2)
            pe.wait_ge(weights_done, 1)

            def turn_tokens(e):
                if e >= 2:
                    pe.wait_ge(xet_done, e - 1)
                for i in range(2):
                    pe.wait_ge(gathered[2 * e + i], 16)
                    mm = pe.transpose(ps_x[e % 2][:, 128 * i:128 * i + 128], xe[:, 2 * e + i, :], ident[:])
                mm.then_inc(xe_turned, 1)

            def up(e, chunks=range(HC)):
                pe.wait_ge(xet_done, e + 1)
                for c in chunks:
                    if e >= 2:
                        pe.wait_ge(gelu_done, HC * (e - 2) + 2 * (c // 2) + 2)
                    pe.matmul(ps_s[2 * (e % 2) + c // 2][:, CAP * (c % 2):CAP * (c % 2) + CAP],
                              w1_sb[:, e, 128 * c:128 * c + 128], xe_t[:, e, :], start=(c % 2 == 0), stop=True,
                              skip_group_check=True).then_inc(up_done, 1)

            def down(e):
                for i in range(2):
                    if e:
                        pe.wait_ge(answer_done, 2 * (e - 1) + i + 1)
                    for c in range(HC):
                        pe.wait_ge(gelu_done, HC * e + c + 1)
                        mm = pe.matmul(ps_y[i][:, 0:E], hid[:, e % 2, c, 128 * i:128 * i + 128],
                                       w2_sb[:, e, c, :], start=(c == 0), stop=(c == HC - 1))
                    mm.then_inc(down_done, 1)

            turn_tokens(0)
            up(0, range(0, HC // 2))
            turn_tokens(1)
            up(0, range(HC // 2, HC))
            for e in range(1, NE + 1):
                if e < NE:
                    up(e)
                if e + 1 < NE:
                    turn_tokens(e + 1)
                down(e - 1)


def kernel(**inputs):
    import numpy as np
    import concourse.bacc as bacc
    from concourse.bass_utils import run_bass_kernel_spmd

    def padded(a):
        a = np.asarray(a)
        wide = np.zeros(a.shape[:-1] + (H, SLOT), a.dtype)
        wide[..., 0:D] = a.reshape(a.shape[:-1] + (H, D))
        return wide.reshape(a.shape[:-1] + (H * SLOT,))

    def both(name, turn=False):
        a, b = np.asarray(inputs["L0_attn_" + name]), np.asarray(inputs["L0_xattn_" + name])
        return np.stack([a, b.T if turn else b])

    def columns(a):
        return a.reshape(2, -1, 128).transpose(2, 0, 1).reshape(128, -1)

    def by_parity(a):
        a = a.reshape(2, PAIRS, 2, D, -1).transpose(2, 1, 3, 0, 4)
        return np.ascontiguousarray(a.reshape(128, 2, -1))

    row = np.arange(128)
    arrays = {
        "x_in": np.ascontiguousarray(np.asarray(inputs["x"]).reshape(NSEQ * S, E)),
        "ctx_in": np.ascontiguousarray(np.asarray(inputs["ctx_1024"]).reshape(NSEQ * S, E)),
        "weights": np.ascontiguousarray(np.concatenate(
            [padded(both("Wq", True)), padded(both("Wk", True)), both("Wv", True)], 2).transpose(1, 0, 2)),
        "columns_in": None, "bo": both("bo"),
    }
    arrays["weights"] = np.concatenate([arrays["weights"], by_parity(both("Wo", True))], 2)
    arrays["columns_in"] = np.concatenate([
        np.eye(128), np.stack([row // SLOT % 2 == 0, row // SLOT % 2 == 1, row % SLOT == D], 1),
        columns(padded(both("bq"))), columns(padded(both("bk"))), by_parity(both("bv"))[..., 0]],
        1).astype(np.float32)
    small = np.concatenate([NE - np.arange(NE), np.arange(NE), np.arange(BLOCKS), np.arange(KT) + 1])
    arrays["consts_in"] = np.concatenate([
        (row[:, None] <= row[None, :]), np.broadcast_to(row + 1, (128, 128)),
        np.broadcast_to(small, (128, small.size)), row[:, None]], 1).astype(np.float32)
    arrays["wg"] = np.asarray(inputs["L0_ffn_Wg"])
    arrays["w1"] = np.asarray(inputs["L0_ffn_W1"])
    arrays["b1"] = np.ascontiguousarray(np.asarray(inputs["L0_ffn_b1"]).reshape(NE, HC, 128).transpose(2, 0, 1))
    arrays["w2"] = np.asarray(inputs["L0_ffn_W2"])
    arrays["b2"] = np.asarray(inputs["L0_ffn_b2"])
    nc = bacc.Bacc("TRN2", target_bir_lowering=False, num_devices=1)
    args = [nc.dram_tensor(n, a.shape, mybir.dt.from_np(a.dtype), kind="ExternalInput").ap()
            for n, a in arrays.items()]
    out = nc.dram_tensor("out", (NSEQ * S, E), F32, kind="ExternalOutput").ap()
    decoder_layer(nc, *args, out)
    r = run_bass_kernel_spmd(nc, [arrays], core_ids=[0])
    return r.results[0]["out"].reshape(NSEQ, S, E)
```
